# Optimizing a Trainium2 kernel written in Bass

```python
import numpy as np
import jax
import jax.numpy as jnp

def _softmax(x, axis=-1):
    return jax.nn.softmax(x, axis=axis)

def _gelu(x):
    return jax.nn.gelu(x, approximate=True)

def _silu(x):
    return jax.nn.silu(x)

def _sigmoid(x):
    return jax.nn.sigmoid(x)

def _layernorm(x, axis=-1, eps=1e-05):
    m = jnp.mean(x, axis=axis, keepdims=True)
    v = jnp.var(x, axis=axis, keepdims=True)
    return (x - m) / jnp.sqrt(v + eps)

def _scatter_add(tgt, idx, src, axis=0):
    return tgt.at[idx].add(src)

def _segment_sum(src, seg, n):
    return jax.ops.segment_sum(src, seg, n)
kernel_name = 'mk_adaln_d2_jaxref_r4_e0c72a'

def setup_inputs(seed: int=0):
    np.random.seed(seed)
    _w = jnp.asarray

    def _L0_attn_setup():
        import jax, jax.numpy as jnp
        import numpy as np
        import math
        D_MODEL, D_C, D_R, NH = (256, 128, 32, 16)
        HD = D_MODEL // NH
        B, T = (2, 512)

        def _rope_tables(T, d_R):
            inv_freq = 1.0 / 10000.0 ** (jnp.arange(0, d_R, 2, dtype=jnp.float32) / d_R)
            t = jnp.arange(T, dtype=jnp.float32)
            freqs = jnp.outer(t, inv_freq)
            return (jnp.cos(freqs), jnp.sin(freqs))

        def _rotary_apply(x, cos, sin):
            d = x.shape[-1]
            x1, x2 = (x[..., :d // 2], x[..., d // 2:])
            return jnp.concatenate([x1 * cos - x2 * sin, x2 * cos + x1 * sin], axis=-1)
        key = jax.random.key(seed)
        ks = jax.random.split(key, 8)
        s = lambda fan_in: 1.0 / math.sqrt(fan_in)
        return {'x': jax.random.normal(ks[0], (B, T, D_MODEL), jnp.float32), 'W_kv_down': jax.random.normal(ks[1], (D_MODEL, D_C), jnp.float32) * s(D_MODEL), 'W_k_up': jax.random.normal(ks[2], (D_C, D_MODEL), jnp.float32) * s(D_C), 'W_v_up': jax.random.normal(ks[3], (D_C, D_MODEL), jnp.float32) * s(D_C), 'W_q': jax.random.normal(ks[4], (D_MODEL, D_MODEL), jnp.float32) * s(D_MODEL), 'W_q_rope': jax.random.normal(ks[5], (D_MODEL, D_R), jnp.float32) * s(D_MODEL), 'W_k_rope': jax.random.normal(ks[6], (D_C, D_R), jnp.float32) * s(D_C), 'W_o': jax.random.normal(ks[7], (D_MODEL, D_MODEL), jnp.float32) * s(D_MODEL)}
    _L0_attn_in = _L0_attn_setup()

    def _L0_ffn_setup():
        import jax, jax.numpy as jnp
        import numpy as np
        K = 2
        key = jax.random.key(seed)
        ks = jax.random.split(key, 9)
        B, S, D, O, E = (4, 256, 256, 256, 8)
        sc = 0.02
        return {'x': jax.random.normal(ks[0], (B, S, D), dtype=jnp.float32), 'gate_w': jax.random.normal(ks[1], (D, E), dtype=jnp.float32) * sc, 'gate_b': jax.random.normal(ks[2], (E,), dtype=jnp.float32) * sc, 'w1': jax.random.normal(ks[3], (E, D, O), dtype=jnp.float32) * sc, 'b1': jax.random.normal(ks[4], (E, O), dtype=jnp.float32) * sc, 'w2': jax.random.normal(ks[5], (E, O, O), dtype=jnp.float32) * sc, 'b2': jax.random.normal(ks[6], (E, O), dtype=jnp.float32) * sc, 'w3': jax.random.normal(ks[7], (E, O, O), dtype=jnp.float32) * sc, 'b3': jax.random.normal(ks[8], (E, O), dtype=jnp.float32) * sc}
    _L0_ffn_in = _L0_ffn_setup()
    _L0_c = _w((lambda *s: np.random.randn(*s).astype(np.float32) * 0.05)(2, 256))
    _L0_wmod = _w((lambda *s: np.random.randn(*s).astype(np.float32) * 0.05)(256, 6 * 256) * 256 ** (-0.5))

    def _L1_attn_setup():
        import jax, jax.numpy as jnp
        import numpy as np
        EMBED_DIM = 256
        NUM_HEADS = 16
        HEAD_DIM = EMBED_DIM // NUM_HEADS
        SCALING = HEAD_DIM ** (-0.5)
        key = jax.random.key(seed)
        k1, k2, k3, k4, k5 = jax.random.split(key, 5)
        B, S, E, H = (2, 512, EMBED_DIM, NUM_HEADS)
        x = jax.random.normal(k1, (B, S, E), dtype=jnp.float32)
        W_A = jax.random.normal(k2, (H, E), dtype=jnp.float32) * E ** (-0.5)
        W_V = jax.random.normal(k3, (E, E), dtype=jnp.float32) * E ** (-0.5)
        W_O = jax.random.normal(k4, (E, E), dtype=jnp.float32) * E ** (-0.5)
        b_O = jax.random.normal(k5, (E,), dtype=jnp.float32) * 0.01
        return {'x': x, 'W_A': W_A, 'W_V': W_V, 'W_O': W_O, 'b_O': b_O}
    _L1_attn_in = _L1_attn_setup()

    def _L1_ffn_setup():
        import jax, jax.numpy as jnp
        import numpy as np
        DIM = 256

        def _reference_tuple_inner(x, W_r, W_k, W_v, mu_r, mu_k):
            B, T, C = x.shape
            x_prev = jnp.concatenate([jnp.zeros((B, 1, C), x.dtype), x[:, :-1, :]], axis=1)
            xr = mu_r * x + (1.0 - mu_r) * x_prev
            xk = mu_k * x + (1.0 - mu_k) * x_prev
            r = jax.nn.sigmoid(jnp.einsum('btc,dc->btd', xr, W_r))
            k = jnp.einsum('btc,dc->btd', xk, W_k)
            k_act = jnp.square(jax.nn.relu(k))
            out = r * jnp.einsum('btc,dc->btd', k_act, W_v)
            new_state = x[:, -1, :]
            return (out, new_state)
        key = jax.random.key(seed)
        ks = jax.random.split(key, 6)
        B, T, C = (8, 512, DIM)
        x = jax.random.normal(ks[0], (B, T, C), dtype=jnp.float32)
        s = 1.0 / np.sqrt(C)
        W_r = jax.random.uniform(ks[1], (C, C), jnp.float32, -s, s)
        W_k = jax.random.uniform(ks[2], (C, C), jnp.float32, -s, s)
        W_v = jax.random.uniform(ks[3], (C, C), jnp.float32, -s, s)
        mu_r = jax.random.uniform(ks[4], (C,), jnp.float32)
        mu_k = jax.random.uniform(ks[5], (C,), jnp.float32)
        return {'x': x, 'W_r': W_r, 'W_k': W_k, 'W_v': W_v, 'mu_r': mu_r, 'mu_k': mu_k}
    _L1_ffn_in = _L1_ffn_setup()
    _L1_c = _w((lambda *s: np.random.randn(*s).astype(np.float32) * 0.05)(2, 256))
    _L1_wmod = _w((lambda *s: np.random.randn(*s).astype(np.float32) * 0.05)(256, 6 * 256) * 256 ** (-0.5))
    _d = {'L0_attn_x': _L0_attn_in['x'], 'L0_attn_W_kv_down': _L0_attn_in['W_kv_down'], 'L0_attn_W_k_up': _L0_attn_in['W_k_up'], 'L0_attn_W_v_up': _L0_attn_in['W_v_up'], 'L0_attn_W_q': _L0_attn_in['W_q'], 'L0_attn_W_q_rope': _L0_attn_in['W_q_rope'], 'L0_attn_W_k_rope': _L0_attn_in['W_k_rope'], 'L0_attn_W_o': _L0_attn_in['W_o'], 'L0_ffn_gate_w': _L0_ffn_in['gate_w'], 'L0_ffn_gate_b': _L0_ffn_in['gate_b'], 'L0_ffn_w1': _L0_ffn_in['w1'], 'L0_ffn_b1': _L0_ffn_in['b1'], 'L0_ffn_w2': _L0_ffn_in['w2'], 'L0_ffn_b2': _L0_ffn_in['b2'], 'L0_ffn_w3': _L0_ffn_in['w3'], 'L0_ffn_b3': _L0_ffn_in['b3'], 'L0_c': _L0_c, 'L0_wmod': _L0_wmod, 'L1_attn_W_A': _L1_attn_in['W_A'], 'L1_attn_W_V': _L1_attn_in['W_V'], 'L1_attn_W_O': _L1_attn_in['W_O'], 'L1_attn_b_O': _L1_attn_in['b_O'], 'L1_ffn_W_r': _L1_ffn_in['W_r'], 'L1_ffn_W_k': _L1_ffn_in['W_k'], 'L1_ffn_W_v': _L1_ffn_in['W_v'], 'L1_ffn_mu_r': _L1_ffn_in['mu_r'], 'L1_ffn_mu_k': _L1_ffn_in['mu_k'], 'L1_c': _L1_c, 'L1_wmod': _L1_wmod}
    _x0 = _d['L0_attn_x']
    _d['L0_attn_x'] = jax.random.normal(jax.random.fold_in(jax.random.key(seed), 1), (2, 2048, 256), dtype=_x0.dtype)
    del _x0
    return _d

def reference(L0_attn_x, L0_attn_W_kv_down, L0_attn_W_k_up, L0_attn_W_v_up, L0_attn_W_q, L0_attn_W_q_rope, L0_attn_W_k_rope, L0_attn_W_o, L0_ffn_gate_w, L0_ffn_gate_b, L0_ffn_w1, L0_ffn_b1, L0_ffn_w2, L0_ffn_b2, L0_ffn_w3, L0_ffn_b3, L0_c, L0_wmod, L1_attn_W_A, L1_attn_W_V, L1_attn_W_O, L1_attn_b_O, L1_ffn_W_r, L1_ffn_W_k, L1_ffn_W_v, L1_ffn_mu_r, L1_ffn_mu_k, L1_c, L1_wmod):

    def _L0_attn_ref(x, W_kv_down, W_k_up, W_v_up, W_q, W_q_rope, W_k_rope, W_o):
        import jax, jax.numpy as jnp
        import numpy as np
        import math
        D_MODEL, D_C, D_R, NH = (256, 128, 32, 16)
        HD = D_MODEL // NH
        B, T = (2, 512)

        def _rope_tables(T, d_R):
            inv_freq = 1.0 / 10000.0 ** (jnp.arange(0, d_R, 2, dtype=jnp.float32) / d_R)
            t = jnp.arange(T, dtype=jnp.float32)
            freqs = jnp.outer(t, inv_freq)
            return (jnp.cos(freqs), jnp.sin(freqs))

        def _rotary_apply(x, cos, sin):
            d = x.shape[-1]
            x1, x2 = (x[..., :d // 2], x[..., d // 2:])
            return jnp.concatenate([x1 * cos - x2 * sin, x2 * cos + x1 * sin], axis=-1)
        Bb, Tt, _ = x.shape
        cos, sin = _rope_tables(Tt, D_R)
        cos = cos[None]
        sin = sin[None]
        c_kv = x @ W_kv_down
        k_rope = _rotary_apply(c_kv @ W_k_rope, cos, sin)
        k = (c_kv @ W_k_up).reshape(Bb, Tt, NH, HD)
        v = (c_kv @ W_v_up).reshape(Bb, Tt, NH, HD)
        q = (x @ W_q).reshape(Bb, Tt, NH, HD)
        q_rope = _rotary_apply(x @ W_q_rope, cos, sin)
        scale = math.sqrt(HD + D_R)
        scores = jnp.einsum('bqhd,bkhd->bhqk', q, k)
        scores = scores + jnp.einsum('bqr,bkr->bqk', q_rope, k_rope)[:, None]
        scores = scores / scale
        causal = jnp.triu(jnp.ones((Tt, Tt), dtype=bool), k=1)
        scores = jnp.where(causal[None, None], -jnp.inf, scores)
        w = jax.nn.softmax(scores, axis=-1)
        attn = jnp.einsum('bhqk,bkhd->bqhd', w, v).reshape(Bb, Tt, D_MODEL)
        return attn @ W_o

    def _L0_ffn_ref(x, gate_w, gate_b, w1, b1, w2, b2, w3, b3):
        import jax, jax.numpy as jnp
        import numpy as np
        K = 2
        E = gate_w.shape[-1]
        logits = jnp.einsum('bsd,de->bse', x, gate_w) + gate_b
        probs = jax.nn.softmax(logits, axis=1)
        vals, idx = jax.lax.top_k(probs, K)
        h = jax.nn.relu(jnp.einsum('bsd,edo->ebso', x, w1) + b1[:, None, None, :])
        h = jax.nn.relu(jnp.einsum('ebso,eop->ebsp', h, w2) + b2[:, None, None, :])
        y = jax.nn.relu(jnp.einsum('ebso,eop->ebsp', h, w3) + b3[:, None, None, :])
        onehot = jax.nn.one_hot(idx, E, dtype=x.dtype)
        w_tok = jnp.einsum('bske,bsk->bse', onehot, vals)
        ind = onehot.max(axis=2)
        v = jnp.einsum('ebso,bse->eo', y, w_tok)
        out = jnp.einsum('bse,eo->bso', ind, v)
        return out

    def _L1_attn_ref(x, W_A, W_V, W_O, b_O):
        import jax, jax.numpy as jnp
        import numpy as np
        EMBED_DIM = 256
        NUM_HEADS = 16
        HEAD_DIM = EMBED_DIM // NUM_HEADS
        SCALING = HEAD_DIM ** (-0.5)
        B, S, E = x.shape
        H, D = (NUM_HEADS, HEAD_DIM)
        z = jnp.einsum('bse,he->bsh', x, W_A) * SCALING
        z = jax.nn.softmax(z, axis=1)
        zp = jnp.transpose(z, (0, 2, 1))
        i = jnp.arange(S)[:, None]
        j = jnp.arange(S)[None, :]
        idx = (i - j) % S
        tril = (j <= i).astype(x.dtype)
        roll = zp[:, :, idx] * tril
        v = jnp.einsum('bse,fe->bsf', x, W_V).reshape(B, S, H, D)
        out = jnp.einsum('bhij,bjhd->bihd', roll, v).reshape(B, S, E)
        return jnp.einsum('bse,fe->bsf', out, W_O) + b_O

    def _L1_ffn_ref(x, W_r, W_k, W_v, mu_r, mu_k):
        import jax, jax.numpy as jnp
        import numpy as np
        DIM = 256

        def _reference_tuple_inner(x, W_r, W_k, W_v, mu_r, mu_k):
            B, T, C = x.shape
            x_prev = jnp.concatenate([jnp.zeros((B, 1, C), x.dtype), x[:, :-1, :]], axis=1)
            xr = mu_r * x + (1.0 - mu_r) * x_prev
            xk = mu_k * x + (1.0 - mu_k) * x_prev
            r = jax.nn.sigmoid(jnp.einsum('btc,dc->btd', xr, W_r))
            k = jnp.einsum('btc,dc->btd', xk, W_k)
            k_act = jnp.square(jax.nn.relu(k))
            out = r * jnp.einsum('btc,dc->btd', k_act, W_v)
            new_state = x[:, -1, :]
            return (out, new_state)
        return _reference_tuple_inner(x, W_r, W_k, W_v, mu_r, mu_k)[0]
    x = L0_attn_x
    mod = (_silu(L0_c) @ L0_wmod).reshape(L0_c.shape[0], 6, 1, -1)
    sa, ca, ga, sb, cb, gb = (mod[:, 0], mod[:, 1], mod[:, 2], mod[:, 3], mod[:, 4], mod[:, 5])
    ga = (2 * (ga >= 0) - 1) * jnp.maximum(jnp.abs(ga), 0.25)
    gb = (2 * (gb >= 0) - 1) * jnp.maximum(jnp.abs(gb), 0.25)
    h = _layernorm(x, axis=-1) * (1 + ca) + sa
    x = x + ga * _L0_attn_ref(h, L0_attn_W_kv_down, L0_attn_W_k_up, L0_attn_W_v_up, L0_attn_W_q, L0_attn_W_q_rope, L0_attn_W_k_rope, L0_attn_W_o)
    h = _layernorm(x, axis=-1) * (1 + cb) + sb
    x = x + gb * _L0_ffn_ref(h, L0_ffn_gate_w, L0_ffn_gate_b, L0_ffn_w1, L0_ffn_b1, L0_ffn_w2, L0_ffn_b2, L0_ffn_w3, L0_ffn_b3)
    mod = (_silu(L1_c) @ L1_wmod).reshape(L1_c.shape[0], 6, 1, -1)
    sa, ca, ga, sb, cb, gb = (mod[:, 0], mod[:, 1], mod[:, 2], mod[:, 3], mod[:, 4], mod[:, 5])
    ga = (2 * (ga >= 0) - 1) * jnp.maximum(jnp.abs(ga), 0.25)
    gb = (2 * (gb >= 0) - 1) * jnp.maximum(jnp.abs(gb), 0.25)
    h = _layernorm(x, axis=-1) * (1 + ca) + sa
    x = x + ga * _L1_attn_ref(h, L1_attn_W_A, L1_attn_W_V, L1_attn_W_O, L1_attn_b_O)
    h = _layernorm(x, axis=-1) * (1 + cb) + sb
    x = x + gb * _L1_ffn_ref(h, L1_ffn_W_r, L1_ffn_W_k, L1_ffn_W_v, L1_ffn_mu_r, L1_ffn_mu_k)
    return x

_drawn_inputs = setup_inputs


def setup_inputs(seed=0):
    import zlib

    import numpy as np

    out = dict(_drawn_inputs(seed))
    spreads = {}
    factors = {'L0_attn_W_k_up': 2.954,
     'L0_attn_W_q': 2.971,
     'L0_attn_W_q_rope': 2.893,
     'L0_attn_W_k_rope': 2.877,
     'L0_ffn_gate_w': 8.0,
     'L0_ffn_gate_b': 200.0,
     'L0_ffn_w1': 8.0,
     'L0_ffn_b1': 8.0,
     'L0_ffn_w2': 8.0,
     'L0_ffn_b2': 8.0,
     'L0_ffn_w3': 8.0,
     'L0_ffn_b3': 25.795,
     'L1_attn_W_A': 8.0,
     'L1_attn_W_V': 8.0,
     'L1_attn_W_O': 8.0,
     'L1_attn_b_O': 200.0,
     'L1_ffn_W_r': 8.0,
     'L1_ffn_W_k': 3.013,
     'L1_ffn_W_v': 2.764,
     'L1_ffn_mu_r': 8.0,
     'L1_ffn_mu_k': 4.998}
    for name, (base, spread) in spreads.items():
        noise = np.random.default_rng([zlib.crc32(name.encode()), seed]).standard_normal(out[name].shape)
        drawn = base * np.exp(spread * noise) if base else spread * noise
        out[name] = jnp.asarray(drawn.astype(out[name].dtype))
    for name, factor in factors.items():
        out[name] = (out[name] * factor).astype(out[name].dtype)
    return out
```

```python
from contextlib import ExitStack

import numpy as np
import concourse.bass as bass
from concourse import mybir

ALU = mybir.AluOpType
ACT = mybir.ActivationFunctionType
AX = mybir.AxisListType
F32 = mybir.dt.float32
F16 = mybir.dt.float16
BF16 = mybir.dt.bfloat16

P = 128
NB = 2
T = 2048
C = 256
KT = C // P
CH = 512
TPC = CH // P
NCH = T // CH
NT = T // P
NH, HD, DR, DC = 16, 16, 32, 128
HG = 4
NG = NH // HG
E = 8
EPS = 1e-5
INV_SCALE = 1.0 / float(np.sqrt(HD + DR))
NEG = -1.0e30
W_LAG = 5
SHIFT_UNIT = 64.0
SA, CA, GA, SB, CB, GB = range(6)


class Shared:

    def __init__(self, inputs, out):
        self.i, self.out = inputs, out


class Chain:

    def __init__(self, eng, sem):
        self.eng, self.sem, self.base, self.n = eng, sem, 0, 0

    def at(self, base):
        self.base, self.n = base, 0

    def link(self, ins):
        ins.then_inc(self.sem, 1)
        self.n += 1
        self.eng.wait_ge(self.sem, self.base + self.n)


def backwards(ap):
    (pstep, pn), (step, n) = ap.ap
    return bass.AP(ap.tensor, ap.offset + (P - 1) * step, [[pstep, pn], [P * step, n // P], [-step, P]])


def ln_rows(dve, chain, x, tile0, hn, ln, b, it):
    for t in range(TPC):
        ins = dve.bn_stats(ln.st[:, t, :], x[:, tile0 + t, :])
    chain.link(ins)
    dve.memset(ln.gap[:, :], 0.0)
    for t in range(TPC):
        ins = dve.bn_aggr(ln.mv[:, t, :], ln.st[:, t, :])
    ins.then_inc(ln.var_ready[b], 1)
    dve.wait_ge(ln.root_ready[b], it + 1)
    chain.link(dve.reciprocal(ln.rs[:, :], ln.sd[:, :]))
    for t in range(TPC):
        ins = dve.tensor_scalar(hn[:, t, :], x[:, tile0 + t, :], ln.mv[:, t, 0:1], ln.rs[:, t:t + 1],
                                ALU.subtract, ALU.mult)
    return ins


def ln_root(act, ln, eps, b, it):
    act.wait_ge(ln.var_ready[b], it + 1)
    act.activation(ln.sd[:, :], ln.mv[:, :, 1], ACT.Sqrt, bias=eps[:, 0:1]).then_inc(ln.root_ready[b], 1)


class LayerNorm:

    def __init__(self, sb, sem):
        self.gap = sb("gap", [1, 1])
        self.st = sb("st", [P, TPC, 6])
        self.mv = sb("mv", [P, TPC, 2])
        self.sd = sb("sd", [P, TPC])
        self.rs = sb("rs", [P, TPC])
        self.var_ready = [sem(f"var_ready{b}") for b in range(NB)]
        self.root_ready = [sem(f"root_ready{b}") for b in range(NB)]


LN_LINKS = 2


def phase_setup(nc, g):
    with ExitStack() as c:
        def sb(n, s, d=F32):
            return c.enter_context(nc.sbuf_tensor("su_" + n, s, d))

        sems = []

        def sem(n):
            sems.append(nc.alloc_semaphore(n))
            return sems[-1]

        wmod = sb("wmod", [P, 2, KT, 6 * C])
        cT = sb("cT", [P, 2, KT, NB])
        ec = sb("ec", [P, 2, KT, NB])
        sc = sb("sc", [P, 2, KT, NB])
        craw = sb("craw", [P, 2, NB, 2, C])
        gabs = sb("gabs", [P, 2, NB, 2, C])
        gsgn = sb("gsgn", [P, 2, NB, 2, C])
        wo0 = sb("wo0", [P, NG, C])
        wo1 = sb("wo1", [P, KT, C])
        bo1 = sb("bo1", [1, C])
        wv1 = sb("wv1", [P, KT, C])
        msk32 = sb("msk32", [P, 2, P])
        s_x = sem("su_x")
        s_ld = sem("su_loads")
        s_exp = sem("su_exp")
        s_silu = sem("su_silu")
        s_mod = sem("su_mod")
        s_gate = sem("su_gate")
        s_gate_free = sem("su_gate_free")
        s_chain = sem("su_chain")
        ps = g.ps
        NLD = 9
        block = c.enter_context(nc.Block())

        @block.sync
        def _(sp):
            sp.dma_start(cT[:, :, :, :], g.i["cT"]).then_inc(s_ld, 16)
            sp.dma_start(wmod[:, 0], g.i["wmod0"].rearrange("(k p) n -> p k n", p=P)).then_inc(s_ld, 16)
            sp.dma_start(g.x[:, 0:NT, :], g.i["x"][0:T, :].rearrange("(t p) c -> p t c", p=P)).then_inc(s_x, 16)
            sp.dma_start(g.x[:, NT:, :], g.i["x"][T:, :].rearrange("(t p) c -> p t c", p=P)).then_inc(s_x, 16)
            sp.dma_start(g.ident[:, :], g.i["ident"]).then_inc(s_ld, 16)
            sp.dma_start(msk32[:, :, :], g.i["mask"]).then_inc(s_ld, 16)
            sp.wait_ge(s_x, 32)

        @block.scalar
        def _(act):
            act.dma_start(wmod[:, 1], g.i["wmod1"].rearrange("(k p) n -> p k n", p=P)).then_inc(s_ld, 16)
            act.dma_start(wo0[:, :, :], g.i["wo0"].rearrange("g p n -> p g n")).then_inc(s_ld, 16)
            act.dma_start(wo1[:, :, :], g.i["wo1"].rearrange("(k p) n -> p k n", p=P)).then_inc(s_ld, 16)
            act.dma_start(bo1[:, :], g.i["bo1"]).then_inc(s_ld, 16)
            act.dma_start(wv1[:, :, :], g.i["wv1"].rearrange("(k p) n -> p k n", p=P)).then_inc(s_ld, 16)
            act.wait_ge(s_ld, 16 * NLD)
            act.activation(ec[:, :, :, :], cT[:, :, :, :], ACT.Exp, scale=-1.0).then_inc(s_exp, 1)

        @block.vector
        def _(dve):
            ch = Chain(dve, s_chain)
            dve.wait_ge(s_ld, 16 * NLD)
            dve.tensor_copy(g.identb[:, :], g.ident[:, :])
            dve.tensor_copy(g.maskb[:, :, :], msk32[:, :, :])
            dve.memset(g.ones1[:, :], 1.0)
            dve.memset(g.eps[:, :], EPS)
            dve.wait_ge(s_exp, 1)
            ch.link(dve.tensor_scalar(ec[:, :, :, :], ec[:, :, :, :], 1.0, None, ALU.add))
            ch.link(dve.reciprocal(sc[:, :, :, :], ec[:, :, :, :]))
            dve.tensor_tensor(sc[:, :, :, :], sc[:, :, :, :], cT[:, :, :, :], ALU.mult).then_inc(s_silu, 1)
            dve.wait_ge(s_mod, 1)
            colp = ps[:, 0, 0:2 * 4 * KT * NB].rearrange("p (l j k b) -> p l j k b", l=2, j=4, k=KT)
            for j in range(4):
                dve.tensor_scalar(g.mod[:, :, j, :, :], colp[:, :, j, :, :], float(j % 2), None, ALU.add)
            for l in range(2):
                for b in range(NB):
                    n = l * NB + b
                    dve.wait_ge(s_gate, n + 1)
                    ch.link(dve.tensor_copy(craw[:, l, b, :, :], ps[:, 1 + n, :].rearrange("p (j c) -> p j c", j=2)))
            ch.link(dve.scalar_tensor_tensor(gabs[:, :, :, :, :], craw[:, :, :, :, :], -1.0, craw[:, :, :, :, :],
                                             ALU.mult, ALU.max))
            ch.link(dve.tensor_scalar(gabs[:, :, :, :, :], gabs[:, :, :, :, :], 0.25, None, ALU.max))
            ch.link(dve.tensor_scalar(gsgn[:, :, :, :, :], craw[:, :, :, :, :], 0.0, 2.0, ALU.is_ge, ALU.mult))
            ch.link(dve.scalar_tensor_tensor(craw[:, :, :, :, :], gsgn[:, :, :, :, :], -1.0, gabs[:, :, :, :, :],
                                             ALU.add, ALU.mult))
            for b in range(NB):
                for k in range(NG):
                    dve.tensor_tensor(g.wog[:, b, k, :], wo0[:, k, :], craw[:, 0, b, 0, :], ALU.mult)
                for k in range(KT):
                    dve.tensor_tensor(g.wo1g[:, b, k, :], wo1[:, k, :], craw[:, 1, b, 0, :], ALU.mult)
                    dve.tensor_tensor(g.wv1g[:, b, k, :], wv1[:, k, :], craw[:, 1, b, 1, :], ALU.mult)
                dve.tensor_tensor(g.bo1g[:, b, :], bo1[:, :], craw[0:1, 1, b, 0, :], ALU.mult)
                dve.tensor_copy(g.gb0[:, b, :], craw[0:E, 0, b, 1, :])

        @block.tensor
        def _(pe):
            pe.wait_ge(s_silu, 1)
            for l in range(2):
                for j, chunk in enumerate((SA, CA, SB, CB)):
                    for k in range(KT):
                        o = ((l * 4 + j) * KT + k) * NB
                        for kk in range(KT):
                            w0 = chunk * C + k * P
                            ins = pe.matmul(ps[:, 0, o:o + NB], wmod[:, l, kk, w0:w0 + P], sc[:, l, kk, :],
                                            start=(kk == 0), stop=(kk == KT - 1))
            ins.then_inc(s_mod, 1)
            for l in range(2):
                for b in range(NB):
                    for j, chunk in enumerate((GA, GB)):
                        for kk in range(KT):
                            ins = pe.matmul(ps[:, 1 + l * NB + b, j * C:(j + 1) * C],
                                            sc[:, l, kk, b:b + 1].to_broadcast([P, P]),
                                            wmod[:, l, kk, chunk * C:(chunk + 1) * C],
                                            start=(kk == 0), stop=(kk == KT - 1))
                    ins.then_inc(s_gate, 1)
    nc.clear_and_free_semaphores(sems)
    nc.all_engine_barrier()


def phase_project(nc, g):
    with ExitStack() as c:
        def sb(n, s, d=F32):
            return c.enter_context(nc.sbuf_tensor("pj_" + n, s, d))

        sems = []

        def sem(n):
            sems.append(nc.alloc_semaphore("pj_" + n))
            return sems[-1]

        ps = g.ps
        wkv = sb("wkv", [P, KT, DC])
        wq = sb("wq", [P, KT, C])
        wqr = sb("wqr", [P, KT, P])
        wkr = sb("wkr", [P, P])
        wku = sb("wku", [P, C])
        wvu = sb("wvu", [P, C])
        cs = sb("cs", [P, T])
        hn = sb("hn", [P, NB, TPC, C])
        ht = sb("ht", [P, NB, KT, CH])
        ckv = sb("ckv", [P, NB, CH])
        hi = sb("hi", [P, NB, 2, KT, CH], F16)
        lo = sb("lo", [P, NB, 2, KT, CH], F16)
        rc = sb("rc", [64, CH])
        rsn = sb("rsn", [64, CH])
        rot = sb("rot", [64, CH])
        roth = sb("roth", [64, NB, 2, CH], F16)
        va = sb("va", [P, NB, TPC, NH, 32])
        w_ld = sem("w_ld")
        ln = LayerNorm(sb, sem)
        chain_s = sem("chain")
        hn_ready = [sem(f"hn_ready{b}") for b in range(NB)]
        tr_done = [sem(f"tr_done{b}") for b in range(NB)]
        ht_ready = [sem(f"ht_ready{b}") for b in range(NB)]
        out_ready = sem("out_ready")
        NBANK = 6
        ckv_ready = [sem(f"ckv_ready{b}") for b in range(NB)]
        hi_ready = [sem(f"hi_ready{b}") for b in range(NB)]
        lo_ready = [sem(f"lo_ready{b}") for b in range(NB)]
        rope_ready = [sem(f"rope_ready{b}") for b in range(NB)]
        va_ready = [sem(f"va_ready{b}") for b in range(NB)]
        stored = [sem(f"stored{b}") for b in range(NB)]
        init_done = sem("init_done")
        NST = 11
        OUTS = ["ckv", "q0", "q1", "qr", "kr", "k0", "k1", "v0", "v1"]
        NO = len(OUTS)

        def slot(b, name):
            n = b * NO + OUTS.index(name)
            return n % NBANK, n // NBANK, n

        def bank(b, name):
            return 2 + slot(b, name)[0]

        block = c.enter_context(nc.Block())

        @block.gpsimd
        def _(pool):
            pool.memset(g.bq[:, :, :], 0.0).then_inc(init_done, 1)
            pool.memset(g.bk[:, :, :], 0.0).then_inc(init_done, 1)
            pool.memset(va[:, :, :, :, HD:32], 1.0).then_inc(init_done, 1)

        @block.sync
        def _(sp):
            for s in (*tr_done, *ht_ready, *stored, *ckv_ready, *rope_ready, *hi_ready, *lo_ready, *va_ready):
                sp.sem_inc(s, 1)
            for dst, src in ((wkv[:, :, :], g.i["wkv"].rearrange("(k p) n -> p k n", p=P)),
                             (wq[:, :, :], g.i["wq"].rearrange("(k p) n -> p k n", p=P)),
                             (wqr[:, :, :], g.i["wqr"].rearrange("(k p) n -> p k n", p=P)),
                             (wkr[:, :], g.i["wkr"]), (wku[:, :], g.i["wku"]), (wvu[:, :], g.i["wvu"]),
                             (cs[:, :], g.i["cs"])):
                sp.dma_start(dst, src).then_inc(w_ld, 16)
            with sp.Fori(0, NCH) as it:
                for b in range(NB):
                    cols = bass.ds(b * T + it * CH, CH)
                    sp.wait_ge(rope_ready[b], 2 * it + 3)
                    sp.dma_start(g.d_qrh[:, cols], roth[0:32, b, 0, :]).then_inc(stored[b], 16)
                    sp.dma_start(g.d_krh[:, cols], roth[0:32, b, 1, :]).then_inc(stored[b], 16)
                    sp.wait_ge(hi_ready[b], 4 * it + 5)
                    sp.wait_ge(lo_ready[b], 4 * it + 5)
                    for n, (dh, dl) in enumerate(((g.d_qh, g.d_ql), (g.d_kh, g.d_kl))):
                        for k in range(KT):
                            sp.dma_start(dh[k * P:(k + 1) * P, cols], hi[:, b, n, k, :]).then_inc(stored[b], 16)
                            sp.dma_start(dl[k * P:(k + 1) * P, cols], lo[:, b, n, k, :]).then_inc(stored[b], 16)
                    sp.wait_ge(va_ready[b], 2 * it + 3)
                    sp.dma_start(g.d_va[:, bass.ds(b * NT + it * TPC, TPC), :],
                                 va[:, b].rearrange("p t h d -> p t (h d)")).then_inc(stored[b], 16)
            for b in range(NB):
                sp.wait_ge(stored[b], 16 * NST * NCH + 1)

        @block.vector
        def _(dve):
            ch = Chain(dve, chain_s)
            links = LN_LINKS + 2 * 3
            dve.wait_ge(w_ld, 16 * 7)
            dve.wait_ge(init_done, 3)
            with dve.Fori(0, NCH) as it:
                for b in range(NB):
                    ch.at((it * NB + b) * links)
                    dve.wait_ge(tr_done[b], 2 * it + 1)
                    ln_rows(dve, ch, g.x, b * NT + it * TPC, hn[:, b], ln, b, it).then_inc(hn_ready[b], 1)
                    dve.wait_ge(stored[b], 16 * NST * it + 1)
                    cols = bass.ds(it * CH, CH)

                    def low(name, n, k, i):
                        dve.wait_ge(hi_ready[b], 4 * it + i + 2)
                        dve.tensor_tensor(lo[:, b, n, k, :], ps[:, bank(b, name), :], hi[:, b, n, k, :],
                                          ALU.subtract).then_inc(lo_ready[b], 1)

                    def rope(name, n):
                        bk, _, o = slot(b, name)
                        dve.wait_ge(out_ready, it * NB * NO + o + 1)
                        dve.tensor_tensor(rc[:, :], ps[0:64, 2 + bk, :], cs[0:64, cols], ALU.mult)
                        ins = dve.tensor_tensor(rsn[:, :], ps[64:128, 2 + bk, :], cs[64:128, cols], ALU.mult)
                        ch.link(ins)
                        ch.link(dve.tensor_tensor(rot[:, :], rc[:, :], rsn[:, :], ALU.add))
                        ch.link(dve.tensor_copy(roth[:, b, n, :], rot[:, :]))
                        r0, r1 = (0, 32) if n == 0 else (32, 0)
                        dst = g.bq if n == 0 else g.bk
                        dve.tensor_tensor(dst[r0:r0 + 32, b, cols], rot[r0:r0 + 32, :], roth[r0:r0 + 32, b, n, :],
                                          ALU.subtract)
                        dve.tensor_copy(dst[r1:r1 + 32, b, cols], roth[r1:r1 + 32, b, n, :]).then_inc(rope_ready[b], 1)

                    low("q0", 0, 0, 0)
                    low("q1", 0, 1, 1)
                    rope("qr", 0)
                    rope("kr", 1)
                    low("k0", 1, 0, 2)
                    low("k1", 1, 1, 3)

        @block.scalar
        def _(act):
            act.wait_ge(init_done, 3)
            with act.Fori(0, NCH) as it:
                for b in range(NB):
                    ln_root(act, ln, g.eps, b, it)
                    for k in range(KT):
                        act.wait_ge(tr_done[b], 2 * it + k + 2)
                        act.activation(ht[:, b, k, :], ps[:, k, :], ACT.Identity, scale=g.mod[:, 0, 1, k, b:b + 1],
                                       bias=g.mod[:, 0, 0, k, b:b + 1]).then_inc(ht_ready[b], 1)

                    def ready(name):
                        bk, _, o = slot(b, name)
                        act.wait_ge(out_ready, it * NB * NO + o + 1)
                        return ps[:, 2 + bk, :]

                    act.activation(ckv[:, b, :], ready("ckv"), ACT.Copy).then_inc(ckv_ready[b], 1)
                    act.wait_ge(stored[b], 16 * NST * it + 1)
                    act.activation(hi[:, b, 0, 0, :], ready("q0"), ACT.Copy).then_inc(hi_ready[b], 1)
                    act.activation(hi[:, b, 0, 1, :], ready("q1"), ACT.Copy).then_inc(hi_ready[b], 1)
                    act.activation(hi[:, b, 1, 0, :], ready("k0"), ACT.Copy).then_inc(hi_ready[b], 1)
                    act.activation(hi[:, b, 1, 1, :], ready("k1"), ACT.Copy).then_inc(hi_ready[b], 1)
                    for j, name in enumerate(("v0", "v1")):
                        act.activation(va[:, b, 2 * j:2 * j + 2, :, 0:HD].rearrange("p t h d -> p (t h) d"),
                                       ready(name).rearrange("p (n d) -> p n d", d=HD),
                                       ACT.Copy).then_inc(va_ready[b], 1)

        @block.tensor
        def _(pe):
            pe.wait_ge(w_ld, 16 * 7)
            with pe.Fori(0, NCH) as it:
                for b in range(NB):
                    pe.wait_ge(hn_ready[b], it + 1)
                    for k in range(KT):
                        pe.wait_ge(ht_ready[1 - b], 2 * it + 2 * b + 1)
                        for t in range(TPC):
                            ins = pe.transpose(ps[:, k, t * P:(t + 1) * P], hn[:, b, t, k * P:(k + 1) * P], g.ident[:, :])
                        ins.then_inc(tr_done[b], 1)

                    def freed(name):
                        bk, turn, _ = slot(b, name)
                        for s, v in readers(bk, turn):
                            pe.wait_ge(s, v + 1)

                    def readers(bk, turn):
                        n = turn * NBANK + bk - NBANK
                        back = 0
                        if n < 0:
                            n += NB * NO
                            back = 1
                        bb, name = n // NO, OUTS[n % NO]
                        i = it + 1 - back
                        if name == "ckv":
                            return [(ckv_ready[bb], i)]
                        if name in ("qr", "kr"):
                            return [(rope_ready[bb], 2 * i - (name == "qr") if not back else 2 * i)]
                        if name in ("q0", "q1", "k0", "k1"):
                            k = ("q0", "q1", "k0", "k1").index(name)
                            return [(lo_ready[bb], 4 * i - 3 + k if not back else 4 * i)]
                        return [(va_ready[bb], 2 * i - (name == "v0") if not back else 2 * i)]

                    pe.wait_ge(ht_ready[b], 2 * it + 3)

                    def product(name, pairs):
                        freed(name)
                        bk, _, _ = slot(b, name)
                        for n, (w, m) in enumerate(pairs):
                            ins = pe.matmul(ps[:, 2 + bk, :], w, m, start=(n == 0), stop=(n == len(pairs) - 1))
                        ins.then_inc(out_ready, 1)

                    h = [ht[:, b, k, :] for k in range(KT)]
                    product("ckv", [(wkv[:, k, :], h[k]) for k in range(KT)])
                    product("q0", [(wq[:, k, 0:P], h[k]) for k in range(KT)])
                    product("q1", [(wq[:, k, P:C], h[k]) for k in range(KT)])
                    product("qr", [(wqr[:, k, :], h[k]) for k in range(KT)])
                    pe.wait_ge(ckv_ready[b], it + 2)
                    product("kr", [(wkr[:, :], ckv[:, b, :])])
                    product("k0", [(wku[:, 0:P], ckv[:, b, :])])
                    product("k1", [(wku[:, P:C], ckv[:, b, :])])
                    for j, name in enumerate(("v0", "v1")):
                        freed(name)
                        bk, _, _ = slot(b, name)
                        for t in range(2):
                            tok = (2 * j + t) * P
                            ins = pe.matmul(ps[:, 2 + bk, t * C:(t + 1) * C], ckv[:, b, tok:tok + P], wvu[:, :],
                                            start=True, stop=True)
                        ins.then_inc(out_ready, 1)
    nc.clear_and_free_semaphores(sems)
    nc.all_engine_barrier()


def attn_steps():
    return [(qc, kb) for qc in reversed(range(NCH)) for kb in range(TPC * (qc + 1))]


def max_items():
    return [(h, qb, j) for qb in range(NT) for h in range(HG) for j in range(qb // TPC + 1)]


def phase_attention(nc, g):
    STEPS, ITEMS = attn_steps(), max_items()
    NS, NI = len(STEPS), len(ITEMS)
    M0, M_END = 4, 36

    def items_of(s):
        if not M0 <= s < M_END:
            return range(0)
        return range(NI * (s - M0) // (M_END - M0), NI * (s + 1 - M0) // (M_END - M0))

    chunk_end = {}
    for n, (qc, kb) in enumerate(STEPS):
        chunk_end[qc] = n
    qcs = list(reversed(range(NCH)))
    o_at = {chunk_end[qc] + 2: i for i, qc in enumerate(qcs)}
    w_at = {chunk_end[qc] + W_LAG + p: (i, p) for i, qc in enumerate(qcs) for p in range(2)}
    PARTS = 4
    r_at = {chunk_end[qc] + 3: i for i, qc in enumerate(qcs)}
    TAIL = max(w_at) + 1 - NS
    LATE = sum(1 for r in w_at if r >= NS)
    TURN = M_END + 1
    W_USES = 2 * NCH
    USES = W_USES + 1
    w_slots = sorted(r % NS for r in w_at)
    m_use = sum(1 for r in w_slots if r <= TURN)

    def uses_before(u, s, late):
        return u * USES + (1 - LATE - late + sum(1 for r in w_slots if r < s) + (1 if s > TURN else 0))

    def events(u, b, s, grp, table):
        found = []
        if s in table:
            found.append((table[s], u, b, grp))
        if NS + s in table and not (isinstance(u, int) and u == 0):
            found.append((table[NS + s], u - 1, 1 - b, grp - (1 - b)))
        return found

    with ExitStack() as c:
        def sb(n, s, d=F32):
            return c.enter_context(nc.sbuf_tensor("at_" + n, s, d))

        def sem(n):
            return c.enter_context(nc.semaphore("at_" + n))

        ps = g.ps
        sq = sb("sq", [P, NB, HG, T], F16)
        sk = sb("sk", [P, NB, HG, T], F16)
        vl = sb("vl", [P, NB, NT, HG * 32])
        pr = sb("pr", [P, 2, 2, 2, CH])
        mx = sb("mx", [P, HG, NT, NCH])
        mm = sb("mm", [P, NB, P])
        mr = sb("mr", [HG * NT, NB, P], F16)
        gap = sb("gap", [1, 1])
        ol = sb("ol", [P, CH])
        oc = sb("oc", [P, CH])
        orc = sb("orc", [P, CH])
        on = sb("on", [P, 2, CH])
        inverted = sem("inverted")
        sums_moved, out_moved = sem("sums_moved"), sem("out_moved")
        init = [sem(f"init{b}") for b in range(NB)]
        once = [sem(f"once{b}") for b in range(NB)]
        ld = [sem(f"ld{b}") for b in range(NB)]
        shift_ld = [sem(f"shift_ld{b}") for b in range(NB)]
        mx_ready, mx_done = sem("mx_ready"), sem("mx_done")
        mm_init, mm_ready, mt_ready = sem("mm_init"), sem("mm_ready"), sem("mt_ready")
        small_free = sem("small_free")
        sc_ready = [sem(f"sc_ready{f}") for f in range(2)]
        exp_done = [sem(f"exp_done{f}") for f in range(2)]
        pv_done = [sem(f"pv_done{f}") for f in range(2)]
        on_ready, w_ready = sem("on_ready"), sem("w_ready")
        O, SMALL, MAXB = 4, 5, 6
        NLD = 7
        masks = g.maskb
        block = c.enter_context(nc.Block())

        def units(eng, body):
            body(0, 0, False)
            with eng.Fori(0, NG - 1) as grp:
                body(grp, 1, False)
                body(grp + 1, 0, False)
            body(NG - 1, 1, True)

        def index(grp, b):
            return grp * NB + b

        @block.gpsimd
        def _(pool):
            for b in range(NB):
                pool.memset(sk[64:P, b, :, :], SHIFT_UNIT).then_inc(init[b], 1)

            def body(grp, b, last):
                u = index(grp, b)
                for i in range(NCH):
                    pool.wait_ge(inverted, (u * NCH + i + 1) * PARTS)
                    if not (isinstance(u, int) and u * NCH + i < 2):
                        pool.wait_ge(w_ready, u * W_USES + 2 * i - 1)
                    pool.wait_ge(out_moved, u * NCH + i + 2)
                    pool.tensor_tensor(on[:, i % 2, :], oc[:, :], orc[:, :], ALU.mult).then_inc(on_ready, 1)
            units(pool, body)

        @block.sync
        def _(sp):
            for s in (*exp_done, on_ready, w_ready, *pv_done, sums_moved, out_moved):
                sp.sem_inc(s, 1)

            def rope(b):
                sp.wait_ge(init[b], 2)
                for h in range(HG):
                    sp.dma_start(sq[16:48, b, h, :], g.d_qrh[:, b * T:(b + 1) * T]).then_inc(once[b], 16)
                    sp.dma_start(sk[16:48, b, h, :], g.d_krh[:, b * T:(b + 1) * T]).then_inc(once[b], 16)

            def load(grp, b):
                rows = bass.ds(grp * (HG * HD), HG * HD)
                cols = slice(b * T, (b + 1) * T)

                def heads(d):
                    return d[rows, cols].rearrange("(h d) n -> d h n", d=HD)
                if not (isinstance(grp, int) and grp == 0):
                    sp.wait_ge(pv_done[(NS - 1) % 2], (index(grp - 1, b) + 1) * (NS // 2) + 1)
                for dst, src in ((sq[0:16, b], g.d_qh), (sk[0:16, b], g.d_kh), (sq[48:64, b], g.d_ql),
                                 (sk[48:64, b], g.d_kh), (sq[64:80, b], g.d_qh), (sk[64:80, b], g.d_kl)):
                    sp.dma_start(dst, heads(src)).then_inc(ld[b], 16)
                sp.dma_start(vl[:, b], g.d_va[:, b * NT:(b + 1) * NT, bass.ds(grp * (HG * 32), HG * 32)])\
                  .then_inc(ld[b], 16)

            def shift(grp, b, use):
                sp.wait_ge(small_free, use)
                sp.dma_start(sq[P - 1:P, b].rearrange("p h (t q) -> p (h t) q", q=P), mr[:, b, :])\
                  .then_inc(shift_ld[b], 16)

            rope(0)
            load(0, 0)
            rope(1)
            load(0, 1)
            shift(0, 0, 1)

            def after(grp, b):
                return uses_before(index(grp, b), TURN, 0) + w_slots.count(TURN) + 1
            with sp.Fori(0, NG - 1) as grp:
                shift(grp, 1, after(grp, 0))
                load(grp + 1, 0)
                shift(grp + 1, 0, after(grp, 1))
                load(grp + 1, 1)
            shift(NG - 1, 1, after(NG - 1, 0))

        @block.tensor
        def _(pe):
            def maxima(v, grp, b, i):
                h, qb, j = ITEMS[i]
                lo, hi_ = j * CH, min(j * CH + CH, (qb + 1) * P)
                bank = MAXB + i % 2
                if not (isinstance(v, int) and v * NI + i - 1 <= 0):
                    pe.wait_ge(mx_done, v * NI + i - 1)
                diag = hi_ == (qb + 1) * P
                ins = pe.matmul(ps[:, bank, 0:hi_ - lo], sq[0:127, b, h, qb * P:(qb + 1) * P], sk[0:127, b, h, lo:hi_],
                                start=True, stop=not diag)
                if diag:
                    ins = pe.matmul(ps[:, bank, hi_ - lo - P:hi_ - lo], g.identb[:, :], masks[:, 1, :],
                                    start=False, stop=True)
                ins.then_inc(mx_ready, 1)

            def turn_maxima(v, b, use):
                pe.wait_ge(mm_ready, v + 1)
                if not (isinstance(use, int) and use == 0):
                    pe.wait_ge(small_free, use)
                pe.transpose(ps[:, SMALL, 0:P], mm[:, b, :], g.ident[:, :]).then_inc(mt_ready, 1)

            pe.wait_ge(once[0], 16 * 2 * HG)
            pe.wait_ge(ld[0], 16 * NLD)
            for i in range(NI):
                maxima(0, 0, 0, i)
            turn_maxima(0, 0, 0)

            def weighted(grp, b, n):
                u = index(grp, b)
                qc, kb = STEPS[n]
                off = max(kb - TPC * qc, 0) * P
                if kb == 0:
                    pe.wait_ge(out_moved, u * NCH + qcs.index(qc) + 1)
                for f in range(2):
                    pe.wait_ge(exp_done[f], u * NS + n + 2)
                for h in range(HG):
                    ins = pe.matmul(ps[32 * h:32 * h + 32, O, off:CH], vl[:, b, kb, 32 * h:32 * h + 32],
                                    pr[:, n % 2, h // 2, h % 2, off:CH], start=(kb == 0),
                                    stop=(kb == TPC * (qc + 1) - 1))
                ins.then_inc(pv_done[n % 2], 1)

            def output(u, b, grp, i, p, use):
                pe.wait_ge(on_ready, u * NCH + i + 2)
                pe.wait_ge(small_free, use)
                for t in range(2):
                    tok = (2 * p + t) * P
                    ins = pe.matmul(ps[:, SMALL, t * C:(t + 1) * C], on[:, i % 2, tok:tok + P],
                                    g.wog[:, b, grp, :], start=True, stop=True)
                ins.then_inc(w_ready, 1)

            def body(grp, b, last):
                u = index(grp, b)
                nxt = (grp, 1) if b == 0 else (grp + 1, 0)
                before = (grp, 0) if b == 1 else (grp - 1, 1)
                first = isinstance(u, int) and u == 0
                pe.wait_ge(shift_ld[b], (grp + 1) * 16)

                def scores(n, h):
                    qc, kb = STEPS[n]
                    t = kb - TPC * qc
                    off = max(t, 0) * P
                    q = slice(qc * CH + off, (qc + 1) * CH)
                    k = slice(kb * P, (kb + 1) * P)
                    f = h // 2
                    if h % 2 == 0:
                        pe.wait_ge(exp_done[f], u * NS + n + 1)
                    ins = pe.matmul(ps[:, h, off:CH], sk[:, b, h, k], sq[:, b, h, q], start=True, stop=False)
                    ins = pe.matmul(ps[:, h, off:CH], g.bk[:, b, k], g.bq[:, b, q], start=False, stop=t < 0)
                    if t >= 0:
                        ins = pe.matmul(ps[:, h, off:off + P], g.identb[:, :], masks[:, 0, :], start=False, stop=True)
                    if h % 2 == 1:
                        ins.then_inc(sc_ready[f], 1)

                for s in range(NS + (TAIL if last else 0)):
                    if s == M0 and not last:
                        if first:
                            pe.wait_ge(once[1], 16 * 2 * HG)
                        pe.wait_ge(ld[nxt[1]], (nxt[0] + 1) * (16 * NLD))
                    items = [] if last else list(items_of(s))
                    for h in range(HG):
                        if items:
                            maxima(u + 1, *nxt, items.pop(0))
                        if s < NS:
                            scores(s, h)
                    for i in items:
                        maxima(u + 1, *nxt, i)
                    if s == 0 and not first:
                        weighted(*before, NS - 1)
                    if 1 <= s <= NS:
                        weighted(grp, b, s - 1)
                    if s < NS:
                        for (i, p), v, vb, vg in events(u, b, s, grp, w_at):
                            output(v, vb, vg, i, p, uses_before(u, s, 1 if last and s > TURN else 0))
                    else:
                        for (i, p), v, vb, vg in events(u + 1, 1 - b, s - NS, grp + b, w_at):
                            output(v, vb, vg, i, p, uses_before(u + 1, s - NS, 1))
                    if s == TURN and not last:
                        turn_maxima(u + 1, nxt[1], uses_before(u, s, 0) + w_slots.count(TURN))

            units(pe, body)

        @block.scalar
        def _(act):
            def move(u, i):
                n_end = chunk_end[qcs[i]]
                act.wait_ge(pv_done[n_end % 2], u * (NS // 2) + n_end // 2 + 2)
                act.wait_ge(on_ready, u * NCH + i + 1)
                act.activation(oc[:, :], ps[:, O, :], ACT.Copy).then_inc(out_moved, 1)

            def body(grp, b, last):
                u = index(grp, b)
                for n, (qc, kb) in enumerate(STEPS):
                    off = max(kb - TPC * qc, 0) * P
                    act.wait_ge(pv_done[n % 2], u * (NS // 2) + n // 2 + 1)
                    for f in range(2):
                        act.wait_ge(sc_ready[f], u * NS + n + 1)
                        act.activation(pr[:, n % 2, f, :, off:CH], ps[:, 2 * f:2 * f + 2, off:CH], ACT.Exp,
                                       scale=INV_SCALE).then_inc(exp_done[f], 1)
                    for (i, v) in [(i, v) for i, v, _, _ in events(u, b, n + 1, grp, o_at)]:
                        move(v, i)
                if last:
                    move(u, NCH - 1)
            units(act, body)

        @block.vector
        def _(dve):
            for b in range(NB):
                dve.memset(sq[64:P, b, :, :], 0.0).then_inc(init[b], 1)
            dve.memset(mm[:, :, :], 0.0).then_inc(mm_init, 1)
            dve.wait_ge(mm_init, 1)

            def maxima(v, i):
                h, qb, j = ITEMS[i]
                width = min(CH, (qb + 1) * P - j * CH)
                dve.wait_ge(mx_ready, v * NI + i + 1)
                dve.tensor_reduce(mx[:, h, qb, j:j + 1], ps[:, MAXB + i % 2, 0:width], AX.X, ALU.max)\
                   .then_inc(mx_done, 1)

            def final(v, b):
                dve.wait_ge(mx_done, v * NI + NI)
                dst = mm[:, b, 0:HG * NT].rearrange("p (h t) -> p h t", h=HG)
                for a in range(NCH):
                    tq = slice(a * TPC, (a + 1) * TPC)
                    ins = dve.tensor_reduce(dst[:, :, tq], mx[:, :, tq, 0:a + 1], AX.X, ALU.max)
                ins.then_inc(mm_ready, 1)

            def negate(v, b):
                dve.wait_ge(mt_ready, v + 1)
                dve.tensor_scalar(mr[:, b, :], ps[0:HG * NT, SMALL, 0:P], -1.0 / SHIFT_UNIT, None, ALU.mult)\
                   .then_inc(small_free, 1)

            for i in range(NI):
                maxima(0, i)
            final(0, 0)
            negate(0, 0)

            def move(u, i):
                dve.wait_ge(out_moved, u * NCH + i + 2)
                dve.wait_ge(on_ready, u * NCH + i + 1)
                dve.memset(gap[:, :], 0.0)
                dve.stream_shuffle(ol[:, :], oc[:, :], [16 + r % 16 for r in range(32)]).then_inc(sums_moved, 1)

            def invert(part, first_after):
                q = slice(part * (CH // PARTS), (part + 1) * (CH // PARTS))
                if first_after is not None:
                    dve.wait_ge(sums_moved, first_after)
                dve.reciprocal(orc[:, q], ol[:, q]).then_inc(inverted, 1)

            def add(u, b, i, p):
                dve.wait_ge(w_ready, u * W_USES + 2 * i + p + 2)
                xs = g.x[:, b * NT + qcs[i] * TPC + 2 * p:b * NT + qcs[i] * TPC + 2 * p + 2, :]
                dve.tensor_tensor(xs, xs, ps[:, SMALL, :].rearrange("p (t c) -> p t c", t=2), ALU.add)\
                   .then_inc(small_free, 1)

            def body(grp, b, last):
                u = index(grp, b)
                nb = 1 - b
                for s in range(NS + (TAIL if last else 0)):
                    here = (u, b, s, grp) if s < NS else (u + 1, 1 - b, s - NS, grp + b)
                    parts = list(range(1, PARTS)) if events(*here, r_at) else []
                    if not last:
                        for n, i in enumerate(items_of(s)):
                            if n and parts:
                                invert(parts.pop(0), None)
                            maxima(u + 1, i)
                    for part in parts:
                        invert(part, None)
                    for i, v, _, _ in events(*here, o_at):
                        move(v, i)
                        invert(0, v * NCH + i + 2)
                    for (i, p), v, vb, _ in events(*here, w_at):
                        add(v, vb, i, p)
                    if s == M_END and not last:
                        final(u + 1, nb)
                    if s == TURN and not last:
                        negate(u + 1, nb)

            units(dve, body)


def phase_route(nc, g):
    with ExitStack() as c:
        def sb(n, s, d=F32):
            return c.enter_context(nc.sbuf_tensor("ro_" + n, s, d))

        def sem(n):
            return c.enter_context(nc.semaphore("ro_" + n))

        ps = g.ps
        hn = sb("hn", [P, NB, TPC, C])
        gw = sb("gw", [P, KT, E])
        gbias = sb("gbias", [E, 1])
        before = sb("before", [P, E, E])
        lg = sb("lg", [E, NB, T])
        nmax = sb("nmax", [E, NB])
        gsum = sb("gsum", [E, NB])
        grec = sb("grec", [E, NB])
        pn = sb("pn", [P, NB * NT, E])
        wins = sb("wins", [P, NB * NT, E, E])
        ties = sb("ties", [P, NB * NT, E, E])
        rank = sb("rank", [P, NB * NT, E])
        wt = sb("wt", [E, NB, T])
        w_ld, chain_s = sem("w_ld"), sem("chain")
        ln = LayerNorm(sb, sem)
        hn_ready = [sem(f"hn_ready{b}") for b in range(NB)]
        tr_done = [sem(f"tr_done{b}") for b in range(NB)]
        ht_ready = [sem(f"ht_ready{b}") for b in range(NB)]
        gate_done = [sem(f"gate_done{b}") for b in range(NB)]
        lg_ready = [sem(f"lg_ready{b}") for b in range(NB)]
        nmax_ready, soft_ready, pr_ready = sem("nmax_ready"), sem("soft_ready"), sem("pr_ready")
        pt_done, ind_ready, it_done, it_ready = sem("pt_done"), sem("ind_ready"), sem("it_done"), sem("it_ready")
        wt_ready, stored = sem("wt_ready"), sem("stored")
        block = c.enter_context(nc.Block())

        @block.sync
        def _(sp):
            for s in (*tr_done, *ht_ready, *lg_ready):
                sp.sem_inc(s, 1)
            sp.dma_start(gw[:, :, :], g.i["gw"].rearrange("(k p) e -> p k e", p=P)).then_inc(w_ld, 16)
            sp.dma_start(gbias[:, :], g.i["gb"]).then_inc(w_ld, 16)
            sp.dma_start(before[:, :, :], g.i["before"]).then_inc(w_ld, 16)
            sp.wait_ge(wt_ready, 1)
            sp.dma_start(g.d_wt, wt[:, :, :].rearrange("e b n -> e (b n)")).then_inc(stored, 16)
            sp.wait_ge(stored, 16)

        @block.vector
        def _(dve):
            ch = Chain(dve, chain_s)
            with dve.Fori(0, NCH) as it:
                for b in range(NB):
                    ch.at((it * NB + b) * LN_LINKS)
                    dve.wait_ge(tr_done[b], 2 * it + 1)
                    ln_rows(dve, ch, g.x, b * NT + it * TPC, hn[:, b], ln, b, it).then_inc(hn_ready[b], 1)
            ch.at(NCH * NB * LN_LINKS)
            dve.wait_ge(w_ld, 48)
            for b in range(NB):
                dve.wait_ge(lg_ready[b], NCH + 1)
                ins = dve.tensor_reduce(nmax[:, b:b + 1], lg[:, b, :], AX.X, ALU.max, negate=True)
                ins.then_inc(nmax_ready, 1)
            dve.wait_ge(soft_ready, NB)
            ch.link(dve.reciprocal(grec[:, :], gsum[:, :]))
            for b in range(NB):
                dve.tensor_scalar(lg[:, b, :], lg[:, b, :], grec[:, b:b + 1], None, ALU.mult).then_inc(pr_ready, 1)
            dve.wait_ge(pt_done, 1)
            ch.link(dve.tensor_copy(pn[:, :, :], ps[:, 0, 0:NB * NT * E].rearrange("p (t e) -> p t e", e=E)))
            shape = [P, NB * NT, E, E]
            mine = pn[:, :, :].unsqueeze(3).to_broadcast(shape)
            other = pn[:, :, :].unsqueeze(2).to_broadcast(shape)
            dve.tensor_tensor(wins[:, :, :, :], other, mine, ALU.is_gt)
            ch.link(dve.tensor_tensor(ties[:, :, :, :], other, mine, ALU.is_equal))
            ch.link(dve.tensor_tensor(ties[:, :, :, :], ties[:, :, :, :],
                                      before[:, :, :].unsqueeze(1).to_broadcast(shape), ALU.mult))
            ch.link(dve.tensor_tensor(wins[:, :, :, :], wins[:, :, :, :], ties[:, :, :, :], ALU.add))
            ch.link(dve.tensor_reduce(rank[:, :, :], wins[:, :, :, :], AX.X, ALU.add))
            dve.tensor_scalar(pn[:, :, :], rank[:, :, :], 2.0, None, ALU.is_lt).then_inc(ind_ready, 1)
            dve.wait_ge(it_ready, NB * NCH)
            dve.tensor_tensor(wt[:, :, :], lg[:, :, :], g.chosen[:, :, :], ALU.mult).then_inc(wt_ready, 1)

        @block.scalar
        def _(act):
            act.wait_ge(w_ld, 48)
            with act.Fori(0, NCH) as it:
                for b in range(NB):
                    cols = bass.ds(b * T + it * CH, CH)
                    ln_root(act, ln, g.eps, b, it)
                    for k in range(KT):
                        act.wait_ge(tr_done[b], 2 * it + k + 2)
                        act.activation(g.ht[:, k, cols], ps[:, k, :], ACT.Identity, scale=g.mod[:, 0, 3, k, b:b + 1],
                                       bias=g.mod[:, 0, 2, k, b:b + 1]).then_inc(ht_ready[b], 1)
                    act.wait_ge(gate_done[b], it + 1)
                    act.activation(lg[:, b, bass.ds(it * CH, CH)], ps[0:E, 2 + b, :], ACT.Identity,
                                   bias=gbias[:, 0:1]).then_inc(lg_ready[b], 1)
            for b in range(NB):
                act.wait_ge(nmax_ready, b + 1)
                act.activation(lg[:, b, :], lg[:, b, :], ACT.Exp, bias=nmax[:, b:b + 1],
                               accum_out=gsum[:, b:b + 1]).then_inc(soft_ready, 1)
            for n in range(NB * NCH):
                act.wait_ge(it_done, n + 1)
                act.activation(g.chosen[:, n // NCH, (n % NCH) * CH:(n % NCH + 1) * CH], ps[0:E, 1 + n % 4, :],
                               ACT.Copy).then_inc(it_ready, 1)

        @block.tensor
        def _(pe):
            pe.wait_ge(w_ld, 48)
            with pe.Fori(0, NCH) as it:
                for b in range(NB):
                    pe.wait_ge(hn_ready[b], it + 1)
                    for k in range(KT):
                        pe.wait_ge(ht_ready[1 - b], 2 * it + 2 * b + 1)
                        for t in range(TPC):
                            ins = pe.transpose(ps[:, k, t * P:(t + 1) * P], hn[:, b, t, k * P:(k + 1) * P], g.ident[:, :])
                        ins.then_inc(tr_done[b], 1)
                    pe.wait_ge(ht_ready[b], 2 * it + 3)
                    pe.wait_ge(lg_ready[b], it + 1)
                    for k in range(KT):
                        ins = pe.matmul(ps[0:E, 2 + b, :], gw[:, k, :], g.ht[:, k, bass.ds(b * T + it * CH, CH)],
                                        start=(k == 0), stop=(k == KT - 1))
                    ins.then_inc(gate_done[b], 1)
            for b in range(NB):
                pe.wait_ge(pr_ready, b + 1)
                for t in range(NT):
                    o = (b * NT + t) * E
                    ins = pe.transpose(ps[:, 0, o:o + E], lg[:, b, t * P:(t + 1) * P], g.ident[0:E, 0:E])
            ins.then_inc(pt_done, 1)
            pe.wait_ge(ind_ready, 1)
            for n in range(NB * NCH):
                if n >= 4:
                    pe.wait_ge(it_ready, n - 3)
                for t in range(TPC):
                    ins = pe.transpose(ps[0:E, 1 + n % 4, t * P:(t + 1) * P], pn[:, n * TPC + t, :], g.ident[:, :])
                ins.then_inc(it_done, 1)


def phase_experts(nc, g):
    with ExitStack() as c:
        def sb(n, s, d=F32):
            return c.enter_context(nc.sbuf_tensor("ex_" + n, s, d))

        def sem(n):
            return c.enter_context(nc.semaphore("ex_" + n))

        ps = g.ps
        w = sb("w", [P, 2, 3, KT, C])
        bias = sb("bias", [P, 2, 3, KT])
        wb = sb("wb", [P, 2, NB * T])
        h1 = sb("h1", [P, 2, KT, CH])
        h2 = sb("h2", [P, 2, KT, CH])
        h3 = sb("h3", [P, 2, KT, CH])
        vacc = sb("vacc", [P, 2, KT, NB * NCH])
        vt = sb("vt", [P, E, KT])
        vtk = sb("vtk", [P, KT, E])
        vg = sb("vg", [E, NB, C])
        NC_ = NB * NCH
        NBODY = 2 * NC_
        ld = [sem(f"ld{p}") for p in range(2)]
        ready = [sem(f"ready{l}") for l in range(3)]
        act_h = [sem(f"act_h{l}") for l in range(2)]
        dve_h = [sem(f"dve_h{l}") for l in range(2)]
        dve_y, act_v = sem("dve_y"), sem("act_v")
        vt_done = [sem(f"vt_done{p}") for p in range(2)]
        chain_s, v_tr, v_ready, o_ready, x_done = (sem("chain"), sem("v_tr"), sem("v_ready"), sem("o_ready"),
                                                   sem("x_done"))
        SEQ = [(l, s - l) for s in range(NBODY + 2) for l in range(3) if 0 <= s - l < NBODY]
        PAIR = {key: n % 4 for n, key in enumerate(SEQ)}
        NLD = 5
        block = c.enter_context(nc.Block())

        @block.sync
        def _(sp):
            for s in (*vt_done, *act_h, *dve_h, dve_y, act_v):
                sp.sem_inc(s, 1)
            with sp.Fori(0, E // 2) as it:
                for p in range(2):
                    e = it * 2 + p
                    sp.wait_ge(vt_done[p], it + 1)
                    for l, src in enumerate((g.i["w1"], g.i["w2"], g.i["w3"])):
                        sp.dma_start(w[:, p, l], src[bass.ds(e, 1)].rearrange("e (k p) o -> p (e k) o", p=P))\
                          .then_inc(ld[p], 16)
                    sp.dma_start(bias[:, p], g.i["b"][bass.ds(e, 1)].rearrange("e p l k -> p (e l) k"))\
                      .then_inc(ld[p], 16)
                    sp.dma_start(wb[:, p, :], g.d_wt[bass.ds(e, 1), :].to_broadcast([P, NB * T])).then_inc(ld[p], 16)

        @block.tensor
        def _(pe):
            with pe.Fori(0, E // 2) as it:
                for n, (l, cc) in enumerate(SEQ):
                    p, chunk = cc // NC_, cc % NC_
                    if l == 0 and chunk == 0:
                        pe.wait_ge(ld[p], (it + 1) * (16 * NLD))
                    left = [0 if n == 0 else None] * 3
                    if n >= 4:
                        left[SEQ[n - 4][0]] = SEQ[n - 4][1] + 1
                    if l:
                        left[l - 1] = max(left[l - 1] or 0, cc + 1)
                    for m in range(3):
                        if left[m] is None:
                            continue
                        if m < 2:
                            pe.wait_ge(act_h[m], it * NBODY + left[m] + 1)
                            pe.wait_ge(dve_h[m], it * NBODY + left[m] + 1)
                        else:
                            pe.wait_ge(dve_y, it * NBODY + left[m] + 1)
                    src = (g.ht[:, :, chunk * CH:(chunk + 1) * CH], h1[:, cc % 2], h2[:, cc % 2])[l]
                    for o in range(KT):
                        for k in range(KT):
                            ins = pe.matmul(ps[:, 2 * PAIR[l, cc] + o, :], w[:, p, l, k, o * P:(o + 1) * P], src[:, k, :],
                                            start=(k == 0), stop=(k == KT - 1))
                    ins.then_inc(ready[l], 1)
            pe.wait_ge(v_ready, 1)
            for k in range(KT):
                ins = pe.transpose(ps[0:E, 0, k * P:(k + 1) * P], vtk[:, k, :], g.ident[:, :])
            ins.then_inc(v_tr, 1)
            for n in range(NB * NT // 2):
                b = n // (NT // 2)
                pe.wait_ge(v_ready, 2 + b)
                if n >= 4:
                    pe.wait_ge(x_done, n - 3)
                for t in range(2):
                    tt = 2 * n + t - b * NT
                    ins = pe.matmul(ps[:, 1 + n % 4, t * C:(t + 1) * C], g.chosen[:, b, tt * P:(tt + 1) * P], vg[:, b, :],
                                    start=True, stop=True)
                ins.then_inc(o_ready, 1)

        @block.scalar
        def _(act):
            with act.Fori(0, E // 2) as it:
                for s in range(NBODY + 3):
                    for l, h in ((0, h1), (1, h2)):
                        cc = s - l
                        if 0 <= cc < NBODY:
                            act.wait_ge(ready[l], it * NBODY + cc + 1)
                            act.activation(h[:, cc % 2, 0, :], ps[:, 2 * PAIR[l, cc], :], ACT.Relu,
                                           bias=bias[:, cc // NC_, l, 0:1]).then_inc(act_h[l], 1)
                    cc = s - 3
                    if 0 <= cc < NBODY:
                        p = cc // NC_
                        if cc % NC_ == 0:
                            act.wait_ge(vt_done[p], it + 1)
                        act.wait_ge(dve_y, it * NBODY + cc + 2)
                        for o in range(KT):
                            ins = act.activation(h3[:, cc % 2, o, :], h3[:, cc % 2, o, :], ACT.Relu,
                                                 accum_out=vacc[:, p, o, cc % NC_:cc % NC_ + 1])
                        ins.then_inc(act_v, 1)

        @block.vector
        def _(dve):
            ch = Chain(dve, chain_s)
            with dve.Fori(0, E // 2) as it:
                for s in range(NBODY + 4):
                    for l, h in ((0, h1), (1, h2)):
                        cc = s - l
                        if 0 <= cc < NBODY:
                            dve.wait_ge(ready[l], it * NBODY + cc + 1)
                            dve.tensor_scalar(h[:, cc % 2, 1, :], ps[:, 2 * PAIR[l, cc] + 1, :],
                                              bias[:, cc // NC_, l, 1:2], 0.0, ALU.add, ALU.max).then_inc(dve_h[l], 1)
                    cc = s - 2
                    if 0 <= cc < NBODY:
                        p, chunk = cc // NC_, cc % NC_
                        dve.wait_ge(ready[2], it * NBODY + cc + 1)
                        dve.wait_ge(act_v, it * NBODY + max(cc - 1, 0) + 1)
                        for o in range(KT):
                            ins = dve.scalar_tensor_tensor(h3[:, cc % 2, o, :], ps[:, 2 * PAIR[2, cc] + o, :],
                                                           bias[:, p, 2, o:o + 1], wb[:, p, chunk * CH:(chunk + 1) * CH],
                                                           ALU.add, ALU.mult)
                        ins.then_inc(dve_y, 1)
                    cc = s - 4
                    if 0 <= cc < NBODY and cc % NC_ == NC_ - 1:
                        p = cc // NC_
                        dve.wait_ge(act_v, it * NBODY + cc + 2)
                        dve.tensor_reduce(vt[:, bass.ds(it * 2 + p, 1), :].rearrange("p e k -> p (e k)"),
                                          vacc[:, p], AX.X, ALU.add).then_inc(vt_done[p], 1)
            dve.wait_ge(vt_done[1], E // 2 + 1)
            dve.tensor_copy(vtk[:, :, :], vt[:, :, :].rearrange("p e k -> p k e")).then_inc(v_ready, 1)
            dve.wait_ge(v_tr, 1)
            for b in range(NB):
                dve.tensor_tensor(vg[:, b, :], ps[0:E, 0, 0:C], g.gb0[:, b, :], ALU.mult).then_inc(v_ready, 1)
            for n in range(NB * NT // 2):
                dve.wait_ge(o_ready, n + 1)
                xs = g.x[:, 2 * n:2 * n + 2, :]
                dve.tensor_tensor(xs, xs, ps[:, 1 + n % 4, :].rearrange("p (t c) -> p t c", t=2), ALU.add)\
                   .then_inc(x_done, 1)


def phase_mix(nc, g):
    with ExitStack() as c:
        def sb(n, s, d=F32):
            return c.enter_context(nc.sbuf_tensor("mi_" + n, s, d))

        def sem(n):
            return c.enter_context(nc.semaphore("mi_" + n))

        ps = g.ps
        hn = sb("hn", [P, NB, TPC, C])
        ht = sb("ht", [P, NB, KT, CH])
        wa = sb("wa", [P, KT, NH])
        wv = sb("wv", [P, KT, C])
        vn = sb("vn", [P, NB * NT, C])
        z = sb("z", [NH, NB, T])
        zero = sb("zero", [NH, NB, P])
        nmax = sb("nmax", [NH, NB])
        zsum = sb("zsum", [NH, NB])
        zrec = sb("zrec", [NH, NB])
        w_ld, chain_s = sem("w_ld"), sem("chain")
        ln = LayerNorm(sb, sem)
        hn_ready = [sem(f"hn_ready{b}") for b in range(NB)]
        tr_done = [sem(f"tr_done{b}") for b in range(NB)]
        ht_ready = [sem(f"ht_ready{b}") for b in range(NB)]
        z_done = [sem(f"z_done{b}") for b in range(NB)]
        z_ready = [sem(f"z_ready{b}") for b in range(NB)]
        v_done = [sem(f"v_done{b}") for b in range(NB)]
        v_ready = [sem(f"v_ready{b}") for b in range(NB)]
        nmax_ready, exp_ready, zn_ready, zstored = sem("nmax_ready"), sem("exp_ready"), sem("zn_ready"), sem("zstored")
        tz = sb("tz", [P, 2, NB, T])
        toep_ld = [[sem(f"toep_ld{p}{b}") for b in range(NB)] for p in range(2)]
        mix_done = [[sem(f"mix_done{p}{b}") for b in range(NB)] for p in range(2)]
        mix_read = [[sem(f"mix_read{p}{b}") for b in range(NB)] for p in range(2)]
        block = c.enter_context(nc.Block())

        @block.gpsimd
        def _(pool):
            pool.memset(zero[:, :, :], 0.0).then_inc(zn_ready, 1)

        @block.sync
        def _(sp):
            for s in (*mix_done[0], *mix_done[1], *tr_done, *ht_ready, *z_ready, *v_ready, *mix_read[0], *mix_read[1]):
                sp.sem_inc(s, 1)
            sp.dma_start(wa[:, :, :], g.i["wa"].rearrange("(k p) h -> p k h", p=P)).then_inc(w_ld, 16)
            sp.dma_start(wv[:, :, :], g.i["wv"].rearrange("(k p) n -> p k n", p=P)).then_inc(w_ld, 16)
            sp.wait_ge(zn_ready, 1 + NB)
            sp.dma_start(g.d_z[:, :, 0:P], zero[:, :, :]).then_inc(zstored, 16)
            sp.dma_start(g.d_z[:, :, P:], z[:, :, :]).then_inc(zstored, 16)
            sp.wait_ge(zstored, 32)
            with sp.Fori(0, NH // 2) as it:
                for p in range(2):
                    for b in range(NB):
                        sp.wait_ge(mix_done[p][b], it + 1)
                        row = g.d_z[bass.ds(it * 2 + p, 1), b, 1:1 + T]
                        src = bass.AP(row.tensor, row.offset, [[1, P], [1, T]])
                        sp.dma_start(tz[:, p, b, :], src).then_inc(toep_ld[p][b], 16)

        @block.vector
        def _(dve):
            ch = Chain(dve, chain_s)
            with dve.Fori(0, NCH) as it:
                for b in range(NB):
                    ch.at((it * NB + b) * LN_LINKS)
                    dve.wait_ge(tr_done[b], 2 * it + 1)
                    ln_rows(dve, ch, g.x, b * NT + it * TPC, hn[:, b], ln, b, it).then_inc(hn_ready[b], 1)
                    for j in range(2):
                        dve.wait_ge(v_done[b], 2 * it + j + 1)
                        dve.tensor_copy(vn[:, bass.ds(b * NT + it * TPC + 2 * j, 2), :],
                                        ps[:, 4 + 2 * b + j, :].rearrange("p (t c) -> p t c", t=2)).then_inc(v_ready[b], 1)
            ch.at(NCH * NB * LN_LINKS)
            for b in range(NB):
                dve.wait_ge(z_ready[b], NCH + 1)
                ins = dve.tensor_reduce(nmax[:, b:b + 1], z[:, b, :], AX.X, ALU.max, negate=True)
                ins.then_inc(nmax_ready, 1)
            dve.wait_ge(exp_ready, NB)
            ch.link(dve.reciprocal(zrec[:, :], zsum[:, :]))
            for b in range(NB):
                dve.tensor_scalar(z[:, b, :], z[:, b, :], zrec[:, b:b + 1], None, ALU.mult).then_inc(zn_ready, 1)
            with dve.Fori(0, NH // 2) as it:
                for p in range(2):
                    for b in range(NB):
                        dve.wait_ge(mix_done[p][b], it + 2)
                        dve.tensor_copy(g.mixed[:, b * NT:(b + 1) * NT, bass.ds((it * 2 + p) * HD, HD)],
                                        ps[:, 2 * p + b, 0:C].rearrange("p (t d) -> p t d", d=HD))\
                           .then_inc(mix_read[p][b], 1)

        @block.scalar
        def _(act):
            with act.Fori(0, NCH) as it:
                for b in range(NB):
                    ln_root(act, ln, g.eps, b, it)
                    for k in range(KT):
                        act.wait_ge(tr_done[b], 2 * it + k + 2)
                        act.activation(backwards(ht[:, b, k, :]), ps[:, k, :].rearrange("p (t n) -> p t n", n=P),
                                       ACT.Identity, scale=g.mod[:, 1, 1, k, b:b + 1],
                                       bias=g.mod[:, 1, 0, k, b:b + 1]).then_inc(ht_ready[b], 1)
                    act.wait_ge(z_done[b], it + 1)
                    act.activation(z[:, b, bass.ds(it * CH, CH)].rearrange("h (t n) -> h t n", n=P),
                                   backwards(ps[0:NH, 2 + b, :]), ACT.Copy,
                                   scale=float(HD) ** -0.5).then_inc(z_ready[b], 1)
            for b in range(NB):
                act.wait_ge(nmax_ready, b + 1)
                act.activation(z[:, b, :], z[:, b, :], ACT.Exp, bias=nmax[:, b:b + 1],
                               accum_out=zsum[:, b:b + 1]).then_inc(exp_ready, 1)

        @block.tensor
        def _(pe):
            pe.wait_ge(w_ld, 32)
            with pe.Fori(0, NCH) as it:
                for b in range(NB):
                    pe.wait_ge(hn_ready[b], it + 1)
                    for k in range(KT):
                        pe.wait_ge(ht_ready[1 - b], 2 * it + 2 * b + 1)
                        for t in range(TPC):
                            ins = pe.transpose(ps[:, k, t * P:(t + 1) * P], hn[:, b, t, k * P:(k + 1) * P], g.ident[:, :])
                        ins.then_inc(tr_done[b], 1)
                    pe.wait_ge(ht_ready[b], 2 * it + 3)
                    pe.wait_ge(z_ready[b], it + 1)
                    for k in range(KT):
                        ins = pe.matmul(ps[0:NH, 2 + b, :], wa[:, k, :], ht[:, b, k, :], start=(k == 0), stop=(k == KT - 1))
                    ins.then_inc(z_done[b], 1)
                    for j in range(2):
                        pe.wait_ge(v_ready[b], 2 * it + j + 1)
                        for t in range(2):
                            tok = (2 * j + t) * P
                            for k in range(KT):
                                ins = pe.matmul(ps[:, 4 + 2 * b + j, t * C:(t + 1) * C], ht[:, b, k, tok:tok + P],
                                                wv[:, k, :], start=(k == 0), stop=(k == KT - 1))
                        ins.then_inc(v_done[b], 1)
            for b in range(NB):
                pe.wait_ge(v_ready[b], 2 * NCH + 1)
            with pe.Fori(0, NH // 2) as it:
                for p in range(2):
                    for b in range(NB):
                        pe.wait_ge(toep_ld[p][b], (it + 1) * 16)
                        pe.wait_ge(mix_read[p][b], it + 1)
                        for d in range(NT):
                            ins = pe.matmul(ps[:, 2 * p + b, d * HD:C], tz[:, p, b, d * P:(d + 1) * P],
                                            vn[:, b * NT:(b + 1) * NT - d, bass.ds((it * 2 + p) * HD, HD)],
                                            start=(d == 0), stop=(d == NT - 1))
                        ins.then_inc(mix_done[p][b], 1)


def phase_mix_out(nc, g):
    with ExitStack() as c:
        def sem(n):
            return c.enter_context(nc.semaphore("mo_" + n))

        ps = g.ps
        at = c.enter_context(nc.sbuf_tensor("mo_at", [P, 2, KT, CH], F32))
        st = c.enter_context(nc.sbuf_tensor("mo_st", [P, NB * NT, 6], F32))
        sd = c.enter_context(nc.sbuf_tensor("mo_sd", [P, NB * NT], F32))
        tr_done, at_ready, o_ready, x_done = sem("tr_done"), sem("at_ready"), sem("o_ready"), sem("x_done")
        st_done, var_ready, root_ready = sem("st_done"), sem("var_ready"), sem("root_ready")
        N = NB * NCH
        block = c.enter_context(nc.Block())

        @block.tensor
        def _(pe):
            def turn(n):
                for k in range(KT):
                    if n:
                        pe.wait_ge(at_ready, KT * (n - 1) + k + 1)
                    for t in range(TPC):
                        ins = pe.transpose(ps[:, k, t * P:(t + 1) * P], g.mixed[:, n * TPC + t, k * P:(k + 1) * P],
                                           g.ident[:, :])
                    ins.then_inc(tr_done, 1)

            turn(0)
            for n in range(N):
                b = n // NCH
                if n + 1 < N:
                    turn(n + 1)
                pe.wait_ge(at_ready, KT * (n + 1))
                for j in range(2):
                    m = 2 * n + j
                    if m >= 4:
                        pe.wait_ge(x_done, m - 3)
                    for t in range(2):
                        tok = (2 * j + t) * P
                        out = ps[:, 2 + m % 4, t * C:(t + 1) * C]
                        for k in range(KT):
                            pe.matmul(out, at[:, n % 2, k, tok:tok + P], g.wo1g[:, b, k, :], start=(k == 0), stop=False)
                        ins = pe.matmul(out, g.ones1[:, :], g.bo1g[:, b, :], start=False, stop=True)
                    ins.then_inc(o_ready, 1)

        @block.scalar
        def _(act):
            for n in range(N):
                if n >= 2:
                    act.wait_ge(o_ready, 2 * (n - 1))
                for k in range(KT):
                    act.wait_ge(tr_done, KT * n + k + 1)
                    act.activation(at[:, n % 2, k, :], ps[:, k, :], ACT.Copy).then_inc(at_ready, 1)
            act.wait_ge(var_ready, 1)
            act.activation(sd[:, :], g.mv[:, :, 1], ACT.Sqrt, bias=g.eps[:, 0:1]).then_inc(root_ready, 1)

        @block.vector
        def _(dve):
            for m in range(2 * N):
                dve.wait_ge(o_ready, m + 1)
                xs = g.x[:, 2 * m:2 * m + 2, :]
                dve.tensor_tensor(xs, xs, ps[:, 2 + m % 4, :].rearrange("p (t c) -> p t c", t=2), ALU.add)\
                   .then_inc(x_done, 1)
                dve.wait_ge(x_done, m + 1)
                for t in range(2 * m, 2 * m + 2):
                    ins = dve.bn_stats(st[:, t, :], g.x[:, t, :])
            ins.then_inc(st_done, 1)
            dve.wait_ge(st_done, 1)
            for t in range(NB * NT):
                ins = dve.bn_aggr(g.mv[:, t, :], st[:, t, :])
            ins.then_inc(var_ready, 1)
            dve.wait_ge(root_ready, 1)
            dve.reciprocal(g.rs[:, :], sd[:, :])


def phase_ffn(nc, g):
    with ExitStack() as c:
        def sb(n, s, d=F32):
            return c.enter_context(nc.sbuf_tensor("ff_" + n, s, d))

        def sem(n):
            return c.enter_context(nc.semaphore("ff_" + n))

        ps = g.ps
        hn = sb("hn", [P, NB, TPC, C])
        ht = sb("ht", [P, NB, KT, CH + 1])
        wr = sb("wr", [P, KT, C])
        wk = sb("wk", [P, KT, C])
        mu = sb("mu", [P, 2, KT])
        omu = sb("omu", [P, 2, KT])
        xp = sb("xp", [P, 2, KT, CH])
        xm = sb("xm", [P, NB, 2, KT, CH])
        r = sb("r", [P, NB, TPC, C])
        kr = sb("kr", [P, NB, KT, CH])
        ka = sb("ka", [P, NB, KT, CH])
        y = sb("y", [P, NB, TPC, C])
        w_ld, chain_s, zero_done = sem("w_ld"), sem("chain"), sem("zero_done")
        hn_ready = [sem(f"hn_ready{b}") for b in range(NB)]
        tr_done = [sem(f"tr_done{b}") for b in range(NB)]
        ht_ready = [sem(f"ht_ready{b}") for b in range(NB)]
        xm_ready = [sem(f"xm_ready{b}") for b in range(NB)]
        r_done = [sem(f"r_done{b}") for b in range(NB)]
        r_ready = [sem(f"r_ready{b}") for b in range(NB)]
        k_done = [sem(f"k_done{b}") for b in range(NB)]
        kr_ready = [sem(f"kr_ready{b}") for b in range(NB)]
        ka_ready = [sem(f"ka_ready{b}") for b in range(NB)]
        v_done = [sem(f"v_done{b}") for b in range(NB)]
        y_ready = [sem(f"y_ready{b}") for b in range(NB)]
        stored = [sem(f"stored{b}") for b in range(NB)]
        block = c.enter_context(nc.Block())

        @block.gpsimd
        def _(pool):
            pool.memset(ht[:, :, :, CH:CH + 1], 0.0).then_inc(zero_done, 1)
            with pool.Fori(0, NCH) as it:
                for b in range(NB):
                    pool.wait_ge(v_done[b], 2 * it + 1)
                    for k in range(KT):
                        pool.wait_ge(kr_ready[b], 2 * it + k + 2)
                        pool.tensor_tensor(ka[:, b, k, :], kr[:, b, k, :], kr[:, b, k, :], ALU.mult)\
                            .then_inc(ka_ready[b], 1)

        @block.sync
        def _(sp):
            for s in (*tr_done, *v_done, *stored, *xm_ready, *kr_ready, *r_ready, *y_ready, *ht_ready):
                sp.sem_inc(s, 1)
            sp.dma_start(wr[:, :, :], g.i["wr"].rearrange("(k p) n -> p k n", p=P)).then_inc(w_ld, 16)
            sp.dma_start(wk[:, :, :], g.i["wk"].rearrange("(k p) n -> p k n", p=P)).then_inc(w_ld, 16)
            sp.dma_start(mu[:, :, :], g.i["mu"]).then_inc(w_ld, 16)
            with sp.Fori(0, NCH) as it:
                for b in range(NB):
                    sp.wait_ge(y_ready[b], 2 * it + 3)
                    sp.dma_start(g.out[bass.ds(b * T + it * CH, CH), :].rearrange("(t p) c -> p t c", p=P), y[:, b])\
                      .then_inc(stored[b], 16)
            for b in range(NB):
                sp.wait_ge(stored[b], 16 * NCH + 1)

        @block.vector
        def _(dve):
            ch = Chain(dve, chain_s)
            dve.wait_ge(w_ld, 48)
            ch.at(0)
            ch.link(dve.tensor_scalar(omu[:, :, :], mu[:, :, :], -1.0, 1.0, ALU.mult, ALU.add))
            links = 1 + 2
            with dve.Fori(0, NCH) as it:
                for b in range(NB):
                    ch.at((it * NB + b) * links + 1)
                    dve.wait_ge(tr_done[b], 2 * it + 1)
                    for t in range(TPC):
                        tile = b * NT + it * TPC + t
                        ins = dve.tensor_scalar(hn[:, b, t, :], g.x[:, tile, :], g.mv[:, tile, 0:1], g.rs[:, bass.ds(tile, 1)],
                                                ALU.subtract, ALU.mult)
                    ins.then_inc(hn_ready[b], 1)
                    dve.wait_ge(ht_ready[b], 3 * it + 4)
                    for q in range(2):
                        for k in range(KT):
                            ins = dve.tensor_scalar(xp[:, q, k, :], ht[:, b, k, 0:CH], omu[:, q, k:k + 1], None, ALU.mult)
                    ch.link(ins)
                    for q in range(2):
                        for k in range(KT):
                            ins = dve.scalar_tensor_tensor(xm[:, b, q, k, :], ht[:, b, k, 1:CH + 1], mu[:, q, k:k + 1],
                                                           xp[:, q, k, :], ALU.mult, ALU.add)
                    ins.then_inc(xm_ready[b], 1)
                    dve.wait_ge(stored[b], 16 * it + 1)
                    for j in range(2):
                        dve.wait_ge(r_ready[b], 2 * it + j + 2)
                        dve.wait_ge(v_done[b], 2 * it + j + 2)
                        ys = y[:, b, 2 * j:2 * j + 2, :]
                        ch.link(dve.tensor_tensor(ys, r[:, b, 2 * j:2 * j + 2, :],
                                                  ps[:, 4 + j, :].rearrange("p (t c) -> p t c", t=2), ALU.mult))
                        dve.tensor_tensor(ys, ys, g.x[:, bass.ds(b * NT + it * TPC + 2 * j, 2), :], ALU.add)\
                           .then_inc(y_ready[b], 1)

        @block.scalar
        def _(act):
            act.wait_ge(zero_done, 1)
            with act.Fori(0, NCH) as it:
                for b in range(NB):
                    act.wait_ge(xm_ready[b], it + 1)
                    act.activation(ht[:, b, :, 0:1], ht[:, b, :, CH:CH + 1], ACT.Copy).then_inc(ht_ready[b], 1)
                    act.wait_ge(ht_ready[b], 3 * it + 2)
                    for k in range(KT):
                        act.wait_ge(tr_done[b], 2 * it + k + 2)
                        act.activation(ht[:, b, k, 1:CH + 1], ps[:, k, :], ACT.Identity, scale=g.mod[:, 1, 3, k, b:b + 1],
                                       bias=g.mod[:, 1, 2, k, b:b + 1]).then_inc(ht_ready[b], 1)
                    for k in range(KT):
                        act.wait_ge(k_done[b], 2 * it + k + 1)
                        act.activation(kr[:, b, k, :], ps[:, 2 + k, :], ACT.Relu).then_inc(kr_ready[b], 1)
                    for j in range(2):
                        act.wait_ge(r_done[b], 2 * it + j + 1)
                        act.activation(r[:, b, 2 * j:2 * j + 2, :], ps[:, 6 + j, :].rearrange("p (t c) -> p t c", t=2),
                                       ACT.Sigmoid).then_inc(r_ready[b], 1)

        @block.tensor
        def _(pe):
            pe.wait_ge(w_ld, 48)
            with pe.Fori(0, NCH) as it:
                for b in range(NB):
                    o = 1 - b
                    pe.wait_ge(hn_ready[b], it + 1)
                    for k in range(KT):
                        pe.wait_ge(ht_ready[o], 3 * it + 3 * b + 1)
                        for t in range(TPC):
                            ins = pe.transpose(ps[:, k, t * P:(t + 1) * P], hn[:, b, t, k * P:(k + 1) * P], g.ident[:, :])
                        ins.then_inc(tr_done[b], 1)
                    pe.wait_ge(xm_ready[b], it + 2)
                    pe.wait_ge(kr_ready[o], 2 * it + 2 * b + 1)
                    for q in range(KT):
                        for k in range(KT):
                            ins = pe.matmul(ps[:, 2 + q, :], wk[:, k, q * P:(q + 1) * P], xm[:, b, 1, k, :],
                                            start=(k == 0), stop=(k == KT - 1))
                        ins.then_inc(k_done[b], 1)
                    pe.wait_ge(r_ready[o], 2 * it + 2 * b + 1)
                    for j in range(2):
                        for t in range(2):
                            tok = (2 * j + t) * P
                            for k in range(KT):
                                ins = pe.matmul(ps[:, 6 + j, t * C:(t + 1) * C], xm[:, b, 0, k, tok:tok + P],
                                                wr[:, k, :], start=(k == 0), stop=(k == KT - 1))
                        ins.then_inc(r_done[b], 1)
                    pe.wait_ge(ka_ready[b], 2 * it + 2)
                    pe.wait_ge(y_ready[o], 2 * it + 2 * b + 1)
                    for j in range(2):
                        for t in range(2):
                            tok = (2 * j + t) * P
                            for k in range(KT):
                                ins = pe.matmul(ps[:, 4 + j, t * C:(t + 1) * C], ka[:, b, k, tok:tok + P],
                                                g.wv1g[:, b, k, :], start=(k == 0), stop=(k == KT - 1))
                        ins.then_inc(v_done[b], 1)


PHASES = (phase_setup, phase_project, phase_attention, phase_route, phase_experts, phase_mix, phase_mix_out, phase_ffn)


def adaln_two_layers(nc, args, out):
    g = Shared(args, out)
    with ExitStack() as c:
        def sb(n, s, d=F32):
            return c.enter_context(nc.sbuf_tensor(n, s, d))

        def dram(n, s, d):
            return nc.dram_tensor(n, s, d).ap()

        g.ps = c.enter_context(nc.psum_tensor("ps", [P, 8, 512], F32))
        g.x = sb("x", [P, NB * NT, C])
        g.ident = sb("ident", [P, P])
        g.identb = sb("identb", [P, P], BF16)
        g.maskb = sb("maskb", [P, 2, P], BF16)
        g.ones1 = sb("ones1", [1, P])
        g.eps = sb("eps", [P, 1])
        g.mv = sb("mv_all", [P, NB * NT, 2])
        g.rs = sb("rs_all", [P, NB * NT])
        g.mod = sb("mod", [P, 2, 4, KT, NB])
        g.wog = sb("wog", [P, NB, NG, C])
        g.wo1g = sb("wo1g", [P, NB, KT, C])
        g.wv1g = sb("wv1g", [P, NB, KT, C])
        g.bo1g = sb("bo1g", [1, NB, C])
        g.gb0 = sb("gb0", [E, NB, C])
        g.d_qh, g.d_ql = dram("d_qh", [C, NB * T], F16), dram("d_ql", [C, NB * T], F16)
        g.d_kh, g.d_kl = dram("d_kh", [C, NB * T], F16), dram("d_kl", [C, NB * T], F16)
        g.d_qrh = dram("d_qrh", [DR, NB * T], F16)
        g.d_krh = dram("d_krh", [DR, NB * T], F16)
        g.d_va = dram("d_va", [P, NB * NT, NH * 32], F32)
        g.d_wt = dram("d_wt", [E, NB * T], F32)
        g.d_z = dram("d_z", [NH, NB, P + T], F32)
        phase_setup(nc, g)
        with ExitStack() as a:
            g.bq = a.enter_context(nc.sbuf_tensor("bq", [P, NB, T], F16))
            g.bk = a.enter_context(nc.sbuf_tensor("bk", [P, NB, T], F16))
            phase_project(nc, g)
            phase_attention(nc, g)
        with ExitStack() as a:
            g.ht = a.enter_context(nc.sbuf_tensor("ht_all", [P, KT, NB * T], F32))
            g.chosen = a.enter_context(nc.sbuf_tensor("chosen", [E, NB, T], F32))
            phase_route(nc, g)
            phase_experts(nc, g)
        with ExitStack() as a:
            g.mixed = a.enter_context(nc.sbuf_tensor("mixed", [P, NB * NT, C], F32))
            phase_mix(nc, g)
            phase_mix_out(nc, g)
        phase_ffn(nc, g)


def constants():
    i = np.arange(P)
    mask = np.stack([np.where(i[:, None] > i[None, :], NEG, 0.0), np.where(i[None, :] > i[:, None], NEG, 0.0)], 1)
    inv = (1.0 / 10000.0 ** (np.arange(0, DR, 2, dtype=np.float32) / np.float32(DR))).astype(np.float32)
    ang = np.outer(np.arange(T, dtype=np.float32), inv).astype(np.float32)
    cos, sin = np.cos(ang).T, np.sin(ang).T
    cs = np.concatenate([cos, cos, cos, cos, -sin, sin, -sin, sin], 0)
    before = np.broadcast_to(np.arange(E)[None, :] < np.arange(E)[:, None], (P, E, E))
    return {"ident": np.eye(P), "mask": mask, "cs": cs, "before": before}


def layout(w):
    half = DR // 2

    def rope_cols(a):
        s = np.concatenate([a[:, half:], a[:, :half]], 1)
        return np.concatenate([a, a, s, s], 1)

    wo = np.zeros((NG, HG, 32, C), np.float32)
    wo[:, :, :HD] = w["L0_attn_W_o"].reshape(NG, HG, HD, C)
    cT = np.stack([w["L0_c"].T.reshape(KT, P, NB), w["L1_c"].T.reshape(KT, P, NB)]).transpose(2, 0, 1, 3)
    b = np.stack([w["L0_ffn_b1"], w["L0_ffn_b2"], w["L0_ffn_b3"]], 1).reshape(E, 3, KT, P).transpose(0, 3, 1, 2)
    mu = np.stack([w["L1_ffn_mu_r"], w["L1_ffn_mu_k"]]).reshape(2, KT, P).transpose(2, 0, 1)
    return {
        "x": w["L0_attn_x"].reshape(NB * T, C), "cT": cT, "wmod0": w["L0_wmod"], "wmod1": w["L1_wmod"],
        "wkv": w["L0_attn_W_kv_down"], "wq": w["L0_attn_W_q"], "wqr": rope_cols(w["L0_attn_W_q_rope"]),
        "wkr": rope_cols(w["L0_attn_W_k_rope"]), "wku": w["L0_attn_W_k_up"], "wvu": w["L0_attn_W_v_up"],
        "wo0": wo.reshape(NG, P, C), "gw": w["L0_ffn_gate_w"], "gb": w["L0_ffn_gate_b"].reshape(E, 1),
        "w1": w["L0_ffn_w1"], "w2": w["L0_ffn_w2"], "w3": w["L0_ffn_w3"], "b": b,
        "wa": w["L1_attn_W_A"].T, "wv": w["L1_attn_W_V"].T, "wo1": w["L1_attn_W_O"].T,
        "bo1": w["L1_attn_b_O"].reshape(1, C), "wr": w["L1_ffn_W_r"].T, "wk": w["L1_ffn_W_k"].T,
        "wv1": w["L1_ffn_W_v"].T, "mu": mu,
    }


def kernel(**inputs):
    import concourse.bacc as bacc
    from concourse.bass_utils import run_bass_kernel_spmd

    nc = bacc.Bacc("TRN2", target_bir_lowering=False, num_devices=1)
    host = layout({k: np.asarray(v) for k, v in inputs.items()})
    host.update({k: v.astype(np.float32) for k, v in constants().items()})
    arrays, args = {}, {}
    for name, a in host.items():
        arrays["in_" + name] = np.ascontiguousarray(a)
        args[name] = nc.dram_tensor("in_" + name, a.shape, F32, kind="ExternalInput").ap()
    out = nc.dram_tensor("out", (NB * T, C), F32, kind="ExternalOutput").ap()
    adaln_two_layers(nc, args, out)
    r = run_bass_kernel_spmd(nc, [arrays], core_ids=[0])
    return r.results[0]["out"].reshape(NB, T, C)
```

```python
from contextlib import ExitStack

import numpy as np
import concourse.bass as bass
from concourse import mybir

ALU = mybir.AluOpType
ACT = mybir.ActivationFunctionType
AX = mybir.AxisListType
F32 = mybir.dt.float32
F16 = mybir.dt.float16
BF16 = mybir.dt.bfloat16

P = 128
NB = 2
T = 2048
C = 256
KT = C // P
CH = 512
TPC = CH // P
NCH = T // CH
NT = T // P
NH, HD, DR, DC = 16, 16, 32, 128
HG = 4
NG = NH // HG
E = 8
EPS = 1e-5
INV_SCALE = 1.0 / float(np.sqrt(HD + DR))
NEG = -1.0e30
W_LAG = 5
SHIFT_UNIT = 64.0
SA, CA, GA, SB, CB, GB = range(6)


class Shared:

    def __init__(self, inputs, out):
        self.i, self.out = inputs, out


class Chain:

    def __init__(self, eng, sem):
        self.eng, self.sem, self.base, self.n = eng, sem, 0, 0

    def at(self, base):
        self.base, self.n = base, 0

    def link(self, ins):
        ins.then_inc(self.sem, 1)
        self.n += 1
        self.eng.wait_ge(self.sem, self.base + self.n)


def backwards(ap):
    (pstep, pn), (step, n) = ap.ap
    return bass.AP(ap.tensor, ap.offset + (P - 1) * step, [[pstep, pn], [P * step, n // P], [-step, P]])


def ln_rows(dve, chain, x, tile0, hn, ln, b, it):
    for t in range(TPC):
        ins = dve.bn_stats(ln.st[:, t, :], x[:, tile0 + t, :])
    chain.link(ins)
    dve.memset(ln.gap[:, :], 0.0)
    for t in range(TPC):
        ins = dve.bn_aggr(ln.mv[:, t, :], ln.st[:, t, :])
    ins.then_inc(ln.var_ready[b], 1)
    dve.wait_ge(ln.root_ready[b], it + 1)
    chain.link(dve.reciprocal(ln.rs[:, :], ln.sd[:, :]))
    for t in range(TPC):
        ins = dve.tensor_scalar(hn[:, t, :], x[:, tile0 + t, :], ln.mv[:, t, 0:1], ln.rs[:, t:t + 1],
                                ALU.subtract, ALU.mult)
    return ins


def ln_root(act, ln, eps, b, it):
    act.wait_ge(ln.var_ready[b], it + 1)
    act.activation(ln.sd[:, :], ln.mv[:, :, 1], ACT.Sqrt, bias=eps[:, 0:1]).then_inc(ln.root_ready[b], 1)


class LayerNorm:

    def __init__(self, sb, sem):
        self.gap = sb("gap", [1, 1])
        self.st = sb("st", [P, TPC, 6])
        self.mv = sb("mv", [P, TPC, 2])
        self.sd = sb("sd", [P, TPC])
        self.rs = sb("rs", [P, TPC])
        self.var_ready = [sem(f"var_ready{b}") for b in range(NB)]
        self.root_ready = [sem(f"root_ready{b}") for b in range(NB)]


LN_LINKS = 2


def phase_setup(nc, g):
    with ExitStack() as c:
        def sb(n, s, d=F32):
            return c.enter_context(nc.sbuf_tensor("su_" + n, s, d))

        sems = []

        def sem(n):
            sems.append(nc.alloc_semaphore(n))
            return sems[-1]

        wmod = sb("wmod", [P, 2, KT, 6 * C])
        cT = sb("cT", [P, 2, KT, NB])
        ec = sb("ec", [P, 2, KT, NB])
        sc = sb("sc", [P, 2, KT, NB])
        craw = sb("craw", [P, 2, NB, 2, C])
        gabs = sb("gabs", [P, 2, NB, 2, C])
        gsgn = sb("gsgn", [P, 2, NB, 2, C])
        wo0 = sb("wo0", [P, NG, C])
        wo1 = sb("wo1", [P, KT, C])
        bo1 = sb("bo1", [1, C])
        wv1 = sb("wv1", [P, KT, C])
        msk32 = sb("msk32", [P, 2, P])
        s_x = sem("su_x")
        s_ld = sem("su_loads")
        s_mod_ld = sem("su_mod_ld")
        s_exp = sem("su_exp")
        s_silu = sem("su_silu")
        s_mod = sem("su_mod")
        s_gate = sem("su_gate")
        s_gate_free = sem("su_gate_free")
        s_chain = sem("su_chain")
        ps = g.ps
        NLD = 6
        block = c.enter_context(nc.Block())

        @block.sync
        def _(sp):
            sp.dma_start(cT[:, :, :, :], g.i["cT"]).then_inc(s_mod_ld, 16)
            sp.dma_start(wmod[:, 0], g.i["wmod0"].rearrange("(k p) n -> p k n", p=P)).then_inc(s_mod_ld, 16)
            sp.dma_start(g.ident[:, :], g.i["ident"]).then_inc(s_ld, 16)
            sp.dma_start(msk32[:, :, :], g.i["mask"]).then_inc(s_ld, 16)
            sp.wait_ge(s_ld, 16 * NLD)
            sp.dma_start(g.x[:, 0:NT, :], g.i["x"][0:T, :].rearrange("(t p) c -> p t c", p=P)).then_inc(s_x, 16)
            sp.dma_start(g.x[:, NT:, :], g.i["x"][T:, :].rearrange("(t p) c -> p t c", p=P)).then_inc(s_x, 16)
            sp.wait_ge(s_x, 32)

        @block.scalar
        def _(act):
            act.dma_start(wmod[:, 1], g.i["wmod1"].rearrange("(k p) n -> p k n", p=P)).then_inc(s_mod_ld, 16)
            act.dma_start(wo0[:, :, :], g.i["wo0"].rearrange("g p n -> p g n")).then_inc(s_ld, 16)
            act.dma_start(wo1[:, :, :], g.i["wo1"].rearrange("(k p) n -> p k n", p=P)).then_inc(s_ld, 16)
            act.dma_start(bo1[:, :], g.i["bo1"]).then_inc(s_ld, 16)
            act.dma_start(wv1[:, :, :], g.i["wv1"].rearrange("(k p) n -> p k n", p=P)).then_inc(s_ld, 16)
            act.wait_ge(s_mod_ld, 16 * 3)
            act.activation(ec[:, :, :, :], cT[:, :, :, :], ACT.Exp, scale=-1.0).then_inc(s_exp, 1)

        @block.vector
        def _(dve):
            ch = Chain(dve, s_chain)
            dve.memset(g.ones1[:, :], 1.0)
            dve.memset(g.eps[:, :], EPS)
            dve.wait_ge(s_exp, 1)
            ch.link(dve.tensor_scalar(ec[:, :, :, :], ec[:, :, :, :], 1.0, None, ALU.add))
            ch.link(dve.reciprocal(sc[:, :, :, :], ec[:, :, :, :]))
            dve.tensor_tensor(sc[:, :, :, :], sc[:, :, :, :], cT[:, :, :, :], ALU.mult).then_inc(s_silu, 1)
            dve.wait_ge(s_ld, 16 * NLD)
            dve.tensor_copy(g.identb[:, :], g.ident[:, :])
            dve.tensor_copy(g.maskb[:, :, :], msk32[:, :, :])
            dve.wait_ge(s_mod, 1)
            colp = ps[:, 0, 0:2 * 4 * KT * NB].rearrange("p (l j k b) -> p l j k b", l=2, j=4, k=KT)
            for j in range(4):
                dve.tensor_scalar(g.mod[:, :, j, :, :], colp[:, :, j, :, :], float(j % 2), None, ALU.add)
            for l in range(2):
                for b in range(NB):
                    n = l * NB + b
                    dve.wait_ge(s_gate, n + 1)
                    ch.link(dve.tensor_copy(craw[:, l, b, :, :], ps[:, 1 + n, :].rearrange("p (j c) -> p j c", j=2)))
            ch.link(dve.scalar_tensor_tensor(gabs[:, :, :, :, :], craw[:, :, :, :, :], -1.0, craw[:, :, :, :, :],
                                             ALU.mult, ALU.max))
            ch.link(dve.tensor_scalar(gabs[:, :, :, :, :], gabs[:, :, :, :, :], 0.25, None, ALU.max))
            ch.link(dve.tensor_scalar(gsgn[:, :, :, :, :], craw[:, :, :, :, :], 0.0, 2.0, ALU.is_ge, ALU.mult))
            ch.link(dve.scalar_tensor_tensor(craw[:, :, :, :, :], gsgn[:, :, :, :, :], -1.0, gabs[:, :, :, :, :],
                                             ALU.add, ALU.mult))
            for b in range(NB):
                for k in range(NG):
                    dve.tensor_tensor(g.wog[:, b, k, :], wo0[:, k, :], craw[:, 0, b, 0, :], ALU.mult)
                for k in range(KT):
                    dve.tensor_tensor(g.wo1g[:, b, k, :], wo1[:, k, :], craw[:, 1, b, 0, :], ALU.mult)
                    dve.tensor_tensor(g.wv1g[:, b, k, :], wv1[:, k, :], craw[:, 1, b, 1, :], ALU.mult)
                dve.tensor_tensor(g.bo1g[:, b, :], bo1[:, :], craw[0:1, 1, b, 0, :], ALU.mult)
                dve.tensor_copy(g.gb0[:, b, :], craw[0:E, 0, b, 1, :])

        @block.tensor
        def _(pe):
            pe.wait_ge(s_silu, 1)
            for l in range(2):
                for j, chunk in enumerate((SA, CA, SB, CB)):
                    for k in range(KT):
                        o = ((l * 4 + j) * KT + k) * NB
                        for kk in range(KT):
                            w0 = chunk * C + k * P
                            ins = pe.matmul(ps[:, 0, o:o + NB], wmod[:, l, kk, w0:w0 + P], sc[:, l, kk, :],
                                            start=(kk == 0), stop=(kk == KT - 1))
            ins.then_inc(s_mod, 1)
            for l in range(2):
                for b in range(NB):
                    for j, chunk in enumerate((GA, GB)):
                        for kk in range(KT):
                            ins = pe.matmul(ps[:, 1 + l * NB + b, j * C:(j + 1) * C],
                                            sc[:, l, kk, b:b + 1].to_broadcast([P, P]),
                                            wmod[:, l, kk, chunk * C:(chunk + 1) * C],
                                            start=(kk == 0), stop=(kk == KT - 1))
                    ins.then_inc(s_gate, 1)
    nc.clear_and_free_semaphores(sems)
    nc.all_engine_barrier()


def one_ahead(eng, start, work):
    start(0, 0)
    with eng.Fori(0, NCH - 1) as it:
        work(it, 0, (it, 1))
        work(it, 1, (it + 1, 0))
    work(NCH - 1, 0, (NCH - 1, 1))
    work(NCH - 1, 1, None)


def phase_project(nc, g):
    with ExitStack() as c:
        def sb(n, s, d=F32):
            return c.enter_context(nc.sbuf_tensor("pj_" + n, s, d))

        sems = []

        def sem(n):
            sems.append(nc.alloc_semaphore("pj_" + n))
            return sems[-1]

        ps = g.ps
        wkv = sb("wkv", [P, KT, DC])
        wq = sb("wq", [P, KT, C])
        wqr = sb("wqr", [P, KT, P])
        wkr = sb("wkr", [P, P])
        wku = sb("wku", [P, C])
        wvu = sb("wvu", [P, C])
        cs = sb("cs", [P, T])
        hn = sb("hn", [P, NB, TPC, C])
        ht = sb("ht", [P, NB, KT, CH])
        ckv = sb("ckv", [P, NB, CH])
        hi = sb("hi", [P, NB, 2, KT, CH], F16)
        lo = sb("lo", [P, NB, 2, KT, CH], F16)
        rc = sb("rc", [64, CH])
        rsn = sb("rsn", [64, CH])
        rot = sb("rot", [64, CH])
        roth = sb("roth", [64, NB, 2, CH], F16)
        va = sb("va", [P, NB, TPC, NH, 32])
        w_ld, cs_ld = sem("w_ld"), sem("cs_ld")
        ln = LayerNorm(sb, sem)
        chain_s, chain_l = sem("chain"), sem("chain_l")
        hn_ready = [sem(f"hn_ready{b}") for b in range(NB)]
        tr_done = [sem(f"tr_done{b}") for b in range(NB)]
        ht_ready = [sem(f"ht_ready{b}") for b in range(NB)]
        out_ready = sem("out_ready")
        NBANK = 6
        ckv_ready = [sem(f"ckv_ready{b}") for b in range(NB)]
        hi_ready = [sem(f"hi_ready{b}") for b in range(NB)]
        lo_ready = [sem(f"lo_ready{b}") for b in range(NB)]
        rope_ready = [sem(f"rope_ready{b}") for b in range(NB)]
        va_ready = [sem(f"va_ready{b}") for b in range(NB)]
        stored = [sem(f"stored{b}") for b in range(NB)]
        init_done = sem("init_done")
        NST = 11
        OUTS = ["ckv", "q0", "q1", "qr", "kr", "k0", "k1", "v0", "v1"]
        NO = len(OUTS)

        def slot(b, name):
            n = b * NO + OUTS.index(name)
            return n % NBANK, n // NBANK, n

        def bank(b, name):
            return 2 + slot(b, name)[0]

        block = c.enter_context(nc.Block())

        @block.gpsimd
        def _(pool):
            pool.memset(g.bq[:, :, :], 0.0).then_inc(init_done, 1)
            pool.memset(g.bk[:, :, :], 0.0).then_inc(init_done, 1)
            pool.memset(va[:, :, :, :, HD:32], 1.0).then_inc(init_done, 1)

        @block.sync
        def _(sp):
            for s in (*tr_done, *ht_ready, *stored, *ckv_ready, *rope_ready, *hi_ready, *lo_ready, *va_ready):
                sp.sem_inc(s, 1)
            for dst, src in ((wkv[:, :, :], g.i["wkv"].rearrange("(k p) n -> p k n", p=P)),
                             (wq[:, :, :], g.i["wq"].rearrange("(k p) n -> p k n", p=P)),
                             (wqr[:, :, :], g.i["wqr"].rearrange("(k p) n -> p k n", p=P)),
                             (wkr[:, :], g.i["wkr"]), (wku[:, :], g.i["wku"]), (wvu[:, :], g.i["wvu"])):
                sp.dma_start(dst, src).then_inc(w_ld, 16)
            sp.dma_start(cs[:, :], g.i["cs"]).then_inc(cs_ld, 16)
            with sp.Fori(0, NCH) as it:
                for b in range(NB):
                    cols = bass.ds(b * T + it * CH, CH)
                    sp.wait_ge(rope_ready[b], 2 * it + 3)
                    sp.dma_start(g.d_qrh[:, cols], roth[0:32, b, 0, :]).then_inc(stored[b], 16)
                    sp.dma_start(g.d_krh[:, cols], roth[0:32, b, 1, :]).then_inc(stored[b], 16)
                    sp.wait_ge(hi_ready[b], 4 * it + 5)
                    sp.wait_ge(lo_ready[b], 4 * it + 5)
                    for n, (dh, dl) in enumerate(((g.d_qh, g.d_ql), (g.d_kh, g.d_kl))):
                        for k in range(KT):
                            sp.dma_start(dh[k * P:(k + 1) * P, cols], hi[:, b, n, k, :]).then_inc(stored[b], 16)
                            sp.dma_start(dl[k * P:(k + 1) * P, cols], lo[:, b, n, k, :]).then_inc(stored[b], 16)
                    sp.wait_ge(va_ready[b], 2 * it + 3)
                    sp.dma_start(g.d_va[:, bass.ds(b * NT + it * TPC, TPC), :],
                                 va[:, b].rearrange("p t h d -> p t (h d)")).then_inc(stored[b], 16)
            for b in range(NB):
                sp.wait_ge(stored[b], 16 * NST * NCH + 1)

        @block.vector
        def _(dve):
            ch = Chain(dve, chain_s)
            ch_ln = Chain(dve, chain_l)

            def normalise(it, b):
                ch_ln.at((it * NB + b) * LN_LINKS)
                dve.wait_ge(tr_done[b], 2 * it + 1)
                ln_rows(dve, ch_ln, g.x, b * NT + it * TPC, hn[:, b], ln, b, it).then_inc(hn_ready[b], 1)

            def work(it, b, ahead):
                ch.at((it * NB + b) * (2 * 3))
                dve.wait_ge(stored[b], 16 * NST * it + 1)
                cols = bass.ds(it * CH, CH)

                def low(name, n, k, i):
                    dve.wait_ge(hi_ready[b], 4 * it + i + 2)
                    dve.tensor_tensor(lo[:, b, n, k, :], ps[:, bank(b, name), :], hi[:, b, n, k, :],
                                      ALU.subtract).then_inc(lo_ready[b], 1)

                def rope(name, n):
                    bk, _, o = slot(b, name)
                    dve.wait_ge(out_ready, it * NB * NO + o + 1)
                    dve.tensor_tensor(rc[:, :], ps[0:64, 2 + bk, :], cs[0:64, cols], ALU.mult)
                    ins = dve.tensor_tensor(rsn[:, :], ps[64:128, 2 + bk, :], cs[64:128, cols], ALU.mult)
                    ch.link(ins)
                    ch.link(dve.tensor_tensor(rot[:, :], rc[:, :], rsn[:, :], ALU.add))
                    ch.link(dve.tensor_copy(roth[:, b, n, :], rot[:, :]))
                    r0, r1 = (0, 32) if n == 0 else (32, 0)
                    dst = g.bq if n == 0 else g.bk
                    dve.tensor_tensor(dst[r0:r0 + 32, b, cols], rot[r0:r0 + 32, :], roth[r0:r0 + 32, b, n, :],
                                      ALU.subtract)
                    dve.tensor_copy(dst[r1:r1 + 32, b, cols], roth[r1:r1 + 32, b, n, :]).then_inc(rope_ready[b], 1)

                low("q0", 0, 0, 0)
                low("q1", 0, 1, 1)
                if ahead:
                    normalise(*ahead)
                dve.wait_ge(cs_ld, 16)
                dve.wait_ge(init_done, 3)
                rope("qr", 0)
                rope("kr", 1)
                low("k0", 1, 0, 2)
                low("k1", 1, 1, 3)
            one_ahead(dve, normalise, work)

        @block.scalar
        def _(act):
            def modulated(it, b):
                for k in range(KT):
                    act.wait_ge(tr_done[b], 2 * it + k + 2)
                    act.activation(ht[:, b, k, :], ps[:, k, :], ACT.Identity, scale=g.mod[:, 0, 1, k, b:b + 1],
                                   bias=g.mod[:, 0, 0, k, b:b + 1]).then_inc(ht_ready[b], 1)

            def prepare(it, b):
                ln_root(act, ln, g.eps, b, it)
                modulated(it, b)

            def work(it, b, ahead):
                def ready(name):
                    bk, _, o = slot(b, name)
                    act.wait_ge(out_ready, it * NB * NO + o + 1)
                    return ps[:, 2 + bk, :]

                act.activation(ckv[:, b, :], ready("ckv"), ACT.Copy).then_inc(ckv_ready[b], 1)
                act.wait_ge(stored[b], 16 * NST * it + 1)
                act.activation(hi[:, b, 0, 0, :], ready("q0"), ACT.Copy).then_inc(hi_ready[b], 1)
                act.activation(hi[:, b, 0, 1, :], ready("q1"), ACT.Copy).then_inc(hi_ready[b], 1)
                if ahead:
                    ln_root(act, ln, g.eps, ahead[1], ahead[0])
                act.activation(hi[:, b, 1, 0, :], ready("k0"), ACT.Copy).then_inc(hi_ready[b], 1)
                act.activation(hi[:, b, 1, 1, :], ready("k1"), ACT.Copy).then_inc(hi_ready[b], 1)
                if ahead:
                    modulated(*ahead)
                act.wait_ge(init_done, 3)
                for j, name in enumerate(("v0", "v1")):
                    act.activation(va[:, b, 2 * j:2 * j + 2, :, 0:HD].rearrange("p t h d -> p (t h) d"),
                                   ready(name).rearrange("p (n d) -> p n d", d=HD),
                                   ACT.Copy).then_inc(va_ready[b], 1)
            one_ahead(act, prepare, work)

        @block.tensor
        def _(pe):
            pe.wait_ge(w_ld, 16 * 6)

            def transposes(it, b):
                pe.wait_ge(hn_ready[b], it + 1)
                for k in range(KT):
                    pe.wait_ge(ht_ready[1 - b], 2 * it + 2 * b + 1)
                    for t in range(TPC):
                        ins = pe.transpose(ps[:, k, t * P:(t + 1) * P], hn[:, b, t, k * P:(k + 1) * P], g.ident[:, :])
                    ins.then_inc(tr_done[b], 1)

            def work(it, b, ahead):
                def freed(name):
                    bk, turn, _ = slot(b, name)
                    for s, v in readers(bk, turn):
                        pe.wait_ge(s, v + 1)

                def readers(bk, turn):
                    n = turn * NBANK + bk - NBANK
                    back = 0
                    if n < 0:
                        n += NB * NO
                        back = 1
                    bb, name = n // NO, OUTS[n % NO]
                    i = it + 1 - back
                    if name == "ckv":
                        return [(ckv_ready[bb], i)]
                    if name in ("qr", "kr"):
                        return [(rope_ready[bb], 2 * i - (name == "qr") if not back else 2 * i)]
                    if name in ("q0", "q1", "k0", "k1"):
                        k = ("q0", "q1", "k0", "k1").index(name)
                        return [(lo_ready[bb], 4 * i - 3 + k if not back else 4 * i)]
                    return [(va_ready[bb], 2 * i - (name == "v0") if not back else 2 * i)]

                pe.wait_ge(ht_ready[b], 2 * it + 3)

                def product(name, pairs):
                    freed(name)
                    bk, _, _ = slot(b, name)
                    for n, (w, m) in enumerate(pairs):
                        ins = pe.matmul(ps[:, 2 + bk, :], w, m, start=(n == 0), stop=(n == len(pairs) - 1))
                    ins.then_inc(out_ready, 1)

                h = [ht[:, b, k, :] for k in range(KT)]
                product("ckv", [(wkv[:, k, :], h[k]) for k in range(KT)])
                product("q0", [(wq[:, k, 0:P], h[k]) for k in range(KT)])
                product("q1", [(wq[:, k, P:C], h[k]) for k in range(KT)])
                product("qr", [(wqr[:, k, :], h[k]) for k in range(KT)])
                pe.wait_ge(ckv_ready[b], it + 2)
                product("kr", [(wkr[:, :], ckv[:, b, :])])
                product("k0", [(wku[:, 0:P], ckv[:, b, :])])
                product("k1", [(wku[:, P:C], ckv[:, b, :])])
                if ahead:
                    transposes(*ahead)
                for j, name in enumerate(("v0", "v1")):
                    freed(name)
                    bk, _, _ = slot(b, name)
                    for t in range(2):
                        tok = (2 * j + t) * P
                        ins = pe.matmul(ps[:, 2 + bk, t * C:(t + 1) * C], ckv[:, b, tok:tok + P], wvu[:, :],
                                        start=True, stop=True)
                    ins.then_inc(out_ready, 1)
            one_ahead(pe, transposes, work)
    nc.clear_and_free_semaphores(sems)
    nc.all_engine_barrier()


def attn_steps():
    return [(qc, kb) for qc in reversed(range(NCH)) for kb in range(TPC * (qc + 1))]


def max_items():
    return [(h, qc * TPC + t, j) for qc in reversed(range(NCH)) for t in range(TPC) for h in range(HG)
            for j in range(qc + 1)]


def phase_attention(nc, g):
    STEPS, ITEMS = attn_steps(), max_items()
    NS, NI = len(STEPS), len(ITEMS)
    M0, M_END = 4, 36

    NE = sum(1 for _, qb, _ in ITEMS if qb >= (NCH - 1) * TPC)
    REST_END = 13
    REST_TURN = REST_END + 1

    def items_of(s, first):
        def share(n0, n1, s0, s1):
            return range(n0 + (n1 - n0) * (s - s0) // (s1 - s0), n0 + (n1 - n0) * (s + 1 - s0) // (s1 - s0))
        if first and s < REST_END:
            return [(0, i) for i in share(NE, NI, 0, REST_END)]
        m0 = REST_TURN if first else M0
        return [(1, i) for i in share(0, NI, m0, M_END)] if m0 <= s < M_END else []

    chunk_end = {}
    for n, (qc, kb) in enumerate(STEPS):
        chunk_end[qc] = n
    qcs = list(reversed(range(NCH)))
    o_at = {chunk_end[qc] + 2: i for i, qc in enumerate(qcs)}
    w_at = {chunk_end[qc] + W_LAG + p: (i, p) for i, qc in enumerate(qcs) for p in range(2)}
    PARTS = 4
    r_at = {chunk_end[qc] + 3: i for i, qc in enumerate(qcs)}
    TAIL = max(w_at) + 1 - NS
    LATE = sum(1 for r in w_at if r >= NS)
    TURN = M_END + 1
    W_USES = 2 * NCH
    USES = W_USES + 1
    w_slots = sorted(r % NS for r in w_at)

    def uses_before(u, s, late):
        return u * USES + (2 - LATE - late + sum(1 for r in w_slots if r < s) + (1 if s > TURN else 0))

    def events(u, b, s, grp, table):
        found = []
        if s in table:
            found.append((table[s], u, b, grp))
        if NS + s in table and not (isinstance(u, int) and u == 0):
            found.append((table[NS + s], u - 1, 1 - b, grp - (1 - b)))
        return found

    with ExitStack() as c:
        def sb(n, s, d=F32):
            return c.enter_context(nc.sbuf_tensor("at_" + n, s, d))

        def sem(n):
            return c.enter_context(nc.semaphore("at_" + n))

        ps = g.ps
        sq = sb("sq", [P, NB, HG, T], F16)
        sk = sb("sk", [P, NB, HG, T], F16)
        vl = sb("vl", [P, NB, NT, HG * 32])
        pr = sb("pr", [P, 2, 2, 2, CH])
        mx = sb("mx", [P, HG, NT, NCH])
        mm = sb("mm", [P, NB, P])
        mr = sb("mr", [HG * NT, NB, P], F16)
        gap = sb("gap", [1, 1])
        ol = sb("ol", [P, CH])
        oc = sb("oc", [P, CH])
        orc = sb("orc", [P, CH])
        on = sb("on", [P, 2, CH])
        inverted = sem("inverted")
        sums_moved, out_moved = sem("sums_moved"), sem("out_moved")
        init = [sem(f"init{b}") for b in range(NB)]
        once = [sem(f"once{b}") for b in range(NB)]
        ld = [sem(f"ld{b}") for b in range(NB)]
        shift_ld = [sem(f"shift_ld{b}") for b in range(NB)]
        mx_ready, mx_done = sem("mx_ready"), sem("mx_done")
        mm_init, mm_ready, mt_ready = sem("mm_init"), sem("mm_ready"), sem("mt_ready")
        small_free = sem("small_free")
        sc_ready = [sem(f"sc_ready{f}") for f in range(2)]
        exp_done = [sem(f"exp_done{f}") for f in range(2)]
        pv_done = [sem(f"pv_done{f}") for f in range(2)]
        on_ready, w_ready = sem("on_ready"), sem("w_ready")
        O, SMALL, MAXB = 4, 5, 6
        NLD = 7
        masks = g.maskb
        block = c.enter_context(nc.Block())

        def units(eng, body):
            body(0, 0, False)
            with eng.Fori(0, NG - 1) as grp:
                body(grp, 1, False)
                body(grp + 1, 0, False)
            body(NG - 1, 1, True)

        def index(grp, b):
            return grp * NB + b

        @block.gpsimd
        def _(pool):
            for b in range(NB):
                pool.memset(sk[64:P, b, :, :], SHIFT_UNIT).then_inc(init[b], 1)

            def body(grp, b, last):
                u = index(grp, b)
                for i in range(NCH):
                    pool.wait_ge(inverted, (u * NCH + i + 1) * PARTS)
                    if not (isinstance(u, int) and u * NCH + i < 2):
                        pool.wait_ge(w_ready, u * W_USES + 2 * i - 1)
                    pool.wait_ge(out_moved, u * NCH + i + 2)
                    pool.tensor_tensor(on[:, i % 2, :], oc[:, :], orc[:, :], ALU.mult).then_inc(on_ready, 1)
            units(pool, body)

        @block.sync
        def _(sp):
            for s in (*exp_done, on_ready, w_ready, *pv_done, sums_moved, out_moved):
                sp.sem_inc(s, 1)

            def rope(b):
                for dst, src in ((sq, g.d_qrh), (sk, g.d_krh)):
                    sp.dma_start(dst[16:48, b], src[:, b * T:(b + 1) * T].unsqueeze(1).to_broadcast([DR, HG, T]))\
                      .then_inc(once[b], 16)

            def load(grp, b):
                rows = bass.ds(grp * (HG * HD), HG * HD)
                cols = slice(b * T, (b + 1) * T)

                def heads(d):
                    return d[rows, cols].rearrange("(h d) n -> d h n", d=HD)
                if not (isinstance(grp, int) and grp == 0):
                    sp.wait_ge(pv_done[(NS - 1) % 2], (index(grp - 1, b) + 1) * (NS // 2) + 1)
                for n, (dst, src) in enumerate(((sq[0:16, b], g.d_qh), (sk[0:16, b], g.d_kh), (sq[48:64, b], g.d_ql),
                                                (sk[48:64, b], g.d_kh), (sq[64:80, b], g.d_qh), (sk[64:80, b], g.d_kl))):
                    if n == 4 and isinstance(grp, int) and grp == 0:
                        sp.wait_ge(init[b], 2)
                    sp.dma_start(dst, heads(src)).then_inc(ld[b], 16)
                sp.dma_start(vl[:, b], g.d_va[:, b * NT:(b + 1) * NT, bass.ds(grp * (HG * 32), HG * 32)])\
                  .then_inc(ld[b], 16)

            def shift(grp, b, use):
                sp.wait_ge(small_free, use)
                sp.dma_start(sq[P - 1:P, b].rearrange("p h (t q) -> p (h t) q", q=P), mr[:, b, :])\
                  .then_inc(shift_ld[b], 16)

            rope(0)
            load(0, 0)
            rope(1)
            load(0, 1)
            shift(0, 0, 1)
            sp.wait_ge(small_free, 2)
            rest = (NCH - 1) * TPC
            for h in range(HG):
                sp.dma_start(sq[P - 1:P, 0, h, 0:rest * P].rearrange("p (t q) -> p t q", q=P),
                             mr[h * NT:h * NT + rest, 0, :]).then_inc(shift_ld[0], 16)

            def after(grp, b):
                return uses_before(index(grp, b), TURN, 0) + w_slots.count(TURN) + 1
            with sp.Fori(0, NG - 1) as grp:
                shift(grp, 1, after(grp, 0))
                load(grp + 1, 0)
                shift(grp + 1, 0, after(grp, 1))
                load(grp + 1, 1)
            shift(NG - 1, 1, after(NG - 1, 0))

        @block.tensor
        def _(pe):
            def maxima(v, grp, b, i):
                h, qb, j = ITEMS[i]
                lo, hi_ = j * CH, min(j * CH + CH, (qb + 1) * P)
                bank = MAXB + i % 2
                if not (isinstance(v, int) and v * NI + i - 1 <= 0):
                    pe.wait_ge(mx_done, v * NI + i - 1)
                diag = hi_ == (qb + 1) * P
                ins = pe.matmul(ps[:, bank, 0:hi_ - lo], sq[0:127, b, h, qb * P:(qb + 1) * P], sk[0:127, b, h, lo:hi_],
                                start=True, stop=not diag)
                if diag:
                    ins = pe.matmul(ps[:, bank, hi_ - lo - P:hi_ - lo], g.identb[:, :], masks[:, 1, :],
                                    start=False, stop=True)
                ins.then_inc(mx_ready, 1)

            def turn_maxima(n, b, use):
                pe.wait_ge(mm_ready, n + 1)
                if not (isinstance(use, int) and use == 0):
                    pe.wait_ge(small_free, use)
                pe.transpose(ps[:, SMALL, 0:P], mm[:, b, :], g.ident[:, :]).then_inc(mt_ready, 1)

            pe.wait_ge(once[0], 16 * 2)
            pe.wait_ge(ld[0], 16 * NLD)
            for i in range(NE):
                maxima(0, 0, 0, i)
            turn_maxima(0, 0, 0)

            def weighted(grp, b, n):
                u = index(grp, b)
                qc, kb = STEPS[n]
                off = max(kb - TPC * qc, 0) * P
                if kb == 0:
                    pe.wait_ge(out_moved, u * NCH + qcs.index(qc) + 1)
                for f in range(2):
                    pe.wait_ge(exp_done[f], u * NS + n + 2)
                for h in range(HG):
                    ins = pe.matmul(ps[32 * h:32 * h + 32, O, off:CH], vl[:, b, kb, 32 * h:32 * h + 32],
                                    pr[:, n % 2, h // 2, h % 2, off:CH], start=(kb == 0),
                                    stop=(kb == TPC * (qc + 1) - 1))
                ins.then_inc(pv_done[n % 2], 1)

            def output(u, b, grp, i, p, use):
                pe.wait_ge(on_ready, u * NCH + i + 2)
                pe.wait_ge(small_free, use)
                for t in range(2):
                    tok = (2 * p + t) * P
                    ins = pe.matmul(ps[:, SMALL, t * C:(t + 1) * C], on[:, i % 2, tok:tok + P],
                                    g.wog[:, b, grp, :], start=True, stop=True)
                ins.then_inc(w_ready, 1)

            def body(grp, b, last):
                u = index(grp, b)
                nxt = (grp, 1) if b == 0 else (grp + 1, 0)
                before = (grp, 0) if b == 1 else (grp - 1, 1)
                first = isinstance(u, int) and u == 0
                pe.wait_ge(shift_ld[b], (grp + 1) * 16 + (16 * HG if b == 0 and not first else 0))

                def scores(n, h):
                    qc, kb = STEPS[n]
                    t = kb - TPC * qc
                    off = max(t, 0) * P
                    q = slice(qc * CH + off, (qc + 1) * CH)
                    k = slice(kb * P, (kb + 1) * P)
                    f = h // 2
                    if h % 2 == 0:
                        pe.wait_ge(exp_done[f], u * NS + n + 1)
                    ins = pe.matmul(ps[:, h, off:CH], sk[:, b, h, k], sq[:, b, h, q], start=True, stop=False)
                    ins = pe.matmul(ps[:, h, off:CH], g.bk[:, b, k], g.bq[:, b, q], start=False, stop=t < 0)
                    if t >= 0:
                        ins = pe.matmul(ps[:, h, off:off + P], g.identb[:, :], masks[:, 0, :], start=False, stop=True)
                    if h % 2 == 1:
                        ins.then_inc(sc_ready[f], 1)

                for s in range(NS + (TAIL if last else 0)):
                    if s == M0 and not last:
                        if first:
                            pe.wait_ge(once[1], 16 * 2)
                        pe.wait_ge(ld[nxt[1]], (nxt[0] + 1) * (16 * NLD))
                    items = [] if last else items_of(s, first)
                    if first and s == chunk_end[NCH - 1] + 1:
                        pe.wait_ge(shift_ld[0], 16 + 16 * HG)
                    for h in range(HG):
                        if items:
                            v, i = items.pop(0)
                            maxima(u + v, *(nxt if v else (grp, b)), i)
                        if s < NS:
                            scores(s, h)
                    for v, i in items:
                        maxima(u + v, *(nxt if v else (grp, b)), i)
                    if s == 0 and not first:
                        weighted(*before, NS - 1)
                    if 1 <= s <= NS:
                        weighted(grp, b, s - 1)
                    if s < NS:
                        for (i, p), v, vb, vg in events(u, b, s, grp, w_at):
                            output(v, vb, vg, i, p, uses_before(u, s, 1 if last and s > TURN else 0))
                    else:
                        for (i, p), v, vb, vg in events(u + 1, 1 - b, s - NS, grp + b, w_at):
                            output(v, vb, vg, i, p, uses_before(u + 1, s - NS, 1))
                    if first and s == REST_TURN:
                        turn_maxima(1, 0, 1)
                    if s == TURN and not last:
                        turn_maxima(u + 2, nxt[1], uses_before(u, s, 0) + w_slots.count(TURN))

            units(pe, body)

        @block.scalar
        def _(act):
            def move(u, i):
                n_end = chunk_end[qcs[i]]
                act.wait_ge(pv_done[n_end % 2], u * (NS // 2) + n_end // 2 + 2)
                act.wait_ge(on_ready, u * NCH + i + 1)
                act.activation(oc[:, :], ps[:, O, :], ACT.Copy).then_inc(out_moved, 1)

            def body(grp, b, last):
                u = index(grp, b)
                for n, (qc, kb) in enumerate(STEPS):
                    off = max(kb - TPC * qc, 0) * P
                    act.wait_ge(pv_done[n % 2], u * (NS // 2) + n // 2 + 1)
                    for f in range(2):
                        act.wait_ge(sc_ready[f], u * NS + n + 1)
                        act.activation(pr[:, n % 2, f, :, off:CH], ps[:, 2 * f:2 * f + 2, off:CH], ACT.Exp,
                                       scale=INV_SCALE).then_inc(exp_done[f], 1)
                    for (i, v) in [(i, v) for i, v, _, _ in events(u, b, n + 1, grp, o_at)]:
                        move(v, i)
                if last:
                    move(u, NCH - 1)
            units(act, body)

        @block.vector
        def _(dve):
            for b in range(NB):
                dve.memset(sq[64:P, b, :, :], 0.0).then_inc(init[b], 1)
            dve.memset(mm[:, :, :], 0.0).then_inc(mm_init, 1)
            dve.wait_ge(mm_init, 1)

            def maxima(v, i):
                h, qb, j = ITEMS[i]
                width = min(CH, (qb + 1) * P - j * CH)
                dve.wait_ge(mx_ready, v * NI + i + 1)
                dve.tensor_reduce(mx[:, h, qb, j:j + 1], ps[:, MAXB + i % 2, 0:width], AX.X, ALU.max)\
                   .then_inc(mx_done, 1)

            def final(v, b, chunks, n):
                dve.wait_ge(mx_done, v * NI + n)
                dst = mm[:, b, 0:HG * NT].rearrange("p (h t) -> p h t", h=HG)
                for a in chunks:
                    tq = slice(a * TPC, (a + 1) * TPC)
                    ins = dve.tensor_reduce(dst[:, :, tq], mx[:, :, tq, 0:a + 1], AX.X, ALU.max)
                ins.then_inc(mm_ready, 1)

            def negate(n, b):
                dve.wait_ge(mt_ready, n + 1)
                dve.tensor_scalar(mr[:, b, :], ps[0:HG * NT, SMALL, 0:P], -1.0 / SHIFT_UNIT, None, ALU.mult)\
                   .then_inc(small_free, 1)

            for i in range(NE):
                maxima(0, i)
            final(0, 0, [NCH - 1], NE)
            negate(0, 0)

            def move(u, i):
                dve.wait_ge(out_moved, u * NCH + i + 2)
                dve.wait_ge(on_ready, u * NCH + i + 1)
                dve.memset(gap[:, :], 0.0)
                dve.stream_shuffle(ol[:, :], oc[:, :], [16 + r % 16 for r in range(32)]).then_inc(sums_moved, 1)

            def invert(part, first_after):
                q = slice(part * (CH // PARTS), (part + 1) * (CH // PARTS))
                if first_after is not None:
                    dve.wait_ge(sums_moved, first_after)
                dve.reciprocal(orc[:, q], ol[:, q]).then_inc(inverted, 1)

            def add(u, b, i, p):
                dve.wait_ge(w_ready, u * W_USES + 2 * i + p + 2)
                xs = g.x[:, b * NT + qcs[i] * TPC + 2 * p:b * NT + qcs[i] * TPC + 2 * p + 2, :]
                dve.tensor_tensor(xs, xs, ps[:, SMALL, :].rearrange("p (t c) -> p t c", t=2), ALU.add)\
                   .then_inc(small_free, 1)

            def body(grp, b, last):
                u = index(grp, b)
                nb = 1 - b
                first = isinstance(u, int) and u == 0
                for s in range(NS + (TAIL if last else 0)):
                    here = (u, b, s, grp) if s < NS else (u + 1, 1 - b, s - NS, grp + b)
                    parts = list(range(1, PARTS)) if events(*here, r_at) else []
                    if not last:
                        for n, (v, i) in enumerate(items_of(s, first)):
                            if n and parts:
                                invert(parts.pop(0), None)
                            maxima(u + v, i)
                    for part in parts:
                        invert(part, None)
                    for i, v, _, _ in events(*here, o_at):
                        move(v, i)
                        invert(0, v * NCH + i + 2)
                    for (i, p), v, vb, _ in events(*here, w_at):
                        add(v, vb, i, p)
                    if first and s == REST_END:
                        final(0, 0, range(NCH - 1), NI)
                    if first and s == REST_TURN:
                        dve.wait_ge(shift_ld[0], 16)
                        negate(1, 0)
                    if s == M_END and not last:
                        final(u + 1, nb, range(NCH), NI)
                    if s == TURN and not last:
                        negate(u + 2, nb)

            units(dve, body)


def phase_route(nc, g):
    with ExitStack() as c:
        def sb(n, s, d=F32):
            return c.enter_context(nc.sbuf_tensor("ro_" + n, s, d))

        def sem(n):
            return c.enter_context(nc.semaphore("ro_" + n))

        ps = g.ps
        hn = sb("hn", [P, NB, TPC, C])
        hf = sb("hf", [P, NB, KT, CH])
        one = sb("one", [P, 1, 1])
        one_set = sem("one_set")
        gw = sb("gw", [P, KT, E])
        gbias = sb("gbias", [E, 1])
        before = sb("before", [P, E, E])
        lg = sb("lg", [E, NB, T])
        nmax = sb("nmax", [E, NB])
        gsum = sb("gsum", [E, NB])
        grec = sb("grec", [E, NB])
        pn = sb("pn", [P, NB * NT, E])
        wins = sb("wins", [P, NB * NT, E, E])
        ties = sb("ties", [P, NB * NT, E, E])
        rank = sb("rank", [P, NB * NT, E])
        wt = sb("wt", [E, NB, T])
        w_ld, chain_s = sem("w_ld"), sem("chain")
        ln = LayerNorm(sb, sem)
        hn_ready = [sem(f"hn_ready{b}") for b in range(NB)]
        tr_done = [sem(f"tr_done{b}") for b in range(NB)]
        ht_ready = [sem(f"ht_ready{b}") for b in range(NB)]
        high = [sem(f"high{b}") for b in range(NB)]
        split = [sem(f"split{b}") for b in range(NB)]
        gate_done = [sem(f"gate_done{b}") for b in range(NB)]
        lg_ready = [sem(f"lg_ready{b}") for b in range(NB)]
        nmax_ready, soft_ready, pr_ready = sem("nmax_ready"), sem("soft_ready"), sem("pr_ready")
        pt_done, ind_ready, it_done, it_ready = sem("pt_done"), sem("ind_ready"), sem("it_done"), sem("it_ready")
        wt_ready, stored = sem("wt_ready"), sem("stored")
        block = c.enter_context(nc.Block())

        @block.sync
        def _(sp):
            for s in (*tr_done, *ht_ready, *lg_ready, *split):
                sp.sem_inc(s, 1)
            sp.dma_start(gw[:, :, :], g.i["gw"].rearrange("(k p) e -> p k e", p=P)).then_inc(w_ld, 16)
            sp.dma_start(gbias[:, :], g.i["gb"]).then_inc(w_ld, 16)
            sp.dma_start(before[:, :, :], g.i["before"]).then_inc(w_ld, 16)
            sp.wait_ge(wt_ready, 1)
            sp.dma_start(g.d_wt, wt[:, :, :].rearrange("e b n -> e (b n)")).then_inc(stored, 16)
            sp.wait_ge(stored, 16)

        @block.gpsimd
        def _(pool):
            pool.memset(one[:, :, :], 1.0).then_inc(one_set, 1)
            pool.wait_ge(one_set, 1)
            with pool.Fori(0, NCH) as it:
                for b in range(NB):
                    cols = bass.ds(b * T + it * CH, CH)
                    pool.wait_ge(ht_ready[b], 2 * it + 3)
                    pool.tensor_tensor(g.hh[:, :, cols], hf[:, b], one[:, :, :].to_broadcast([P, KT, CH]), ALU.mult)\
                        .then_inc(high[b], 1)
                    pool.wait_ge(high[b], it + 1)
                    pool.tensor_tensor(g.hl[:, :, cols], hf[:, b], g.hh[:, :, cols], ALU.subtract)\
                        .then_inc(split[b], 1)

        @block.vector
        def _(dve):
            ch = Chain(dve, chain_s)
            with dve.Fori(0, NCH) as it:
                for b in range(NB):
                    ch.at((it * NB + b) * LN_LINKS)
                    dve.wait_ge(tr_done[b], 2 * it + 1)
                    ln_rows(dve, ch, g.x, b * NT + it * TPC, hn[:, b], ln, b, it).then_inc(hn_ready[b], 1)
            ch.at(NCH * NB * LN_LINKS)
            dve.wait_ge(w_ld, 48)
            for b in range(NB):
                dve.wait_ge(lg_ready[b], NCH + 1)
                ins = dve.tensor_reduce(nmax[:, b:b + 1], lg[:, b, :], AX.X, ALU.max, negate=True)
                ins.then_inc(nmax_ready, 1)
            dve.wait_ge(soft_ready, NB)
            ch.link(dve.reciprocal(grec[:, :], gsum[:, :]))
            for b in range(NB):
                dve.tensor_scalar(lg[:, b, :], lg[:, b, :], grec[:, b:b + 1], None, ALU.mult).then_inc(pr_ready, 1)
            dve.wait_ge(pt_done, 1)
            ch.link(dve.tensor_copy(pn[:, :, :], ps[:, 0, 0:NB * NT * E].rearrange("p (t e) -> p t e", e=E)))
            shape = [P, NB * NT, E, E]
            mine = pn[:, :, :].unsqueeze(3).to_broadcast(shape)
            other = pn[:, :, :].unsqueeze(2).to_broadcast(shape)
            dve.tensor_tensor(wins[:, :, :, :], other, mine, ALU.is_gt)
            ch.link(dve.tensor_tensor(ties[:, :, :, :], other, mine, ALU.is_equal))
            ch.link(dve.tensor_tensor(ties[:, :, :, :], ties[:, :, :, :],
                                      before[:, :, :].unsqueeze(1).to_broadcast(shape), ALU.mult))
            ch.link(dve.tensor_tensor(wins[:, :, :, :], wins[:, :, :, :], ties[:, :, :, :], ALU.add))
            ch.link(dve.tensor_reduce(rank[:, :, :], wins[:, :, :, :], AX.X, ALU.add))
            dve.tensor_scalar(pn[:, :, :], rank[:, :, :], 2.0, None, ALU.is_lt).then_inc(ind_ready, 1)
            dve.wait_ge(it_ready, NB * NCH)
            dve.tensor_tensor(wt[:, :, :], lg[:, :, :], g.chosen[:, :, :], ALU.mult).then_inc(wt_ready, 1)

        @block.scalar
        def _(act):
            def prepare(it, b):
                ln_root(act, ln, g.eps, b, it)
                for k in range(KT):
                    act.wait_ge(tr_done[b], 2 * it + k + 2)
                    act.wait_ge(split[b], it + 1)
                    act.activation(hf[:, b, k, :], ps[:, k, :], ACT.Identity, scale=g.mod[:, 0, 3, k, b:b + 1],
                                   bias=g.mod[:, 0, 2, k, b:b + 1]).then_inc(ht_ready[b], 1)

            def work(it, b, ahead):
                if ahead:
                    prepare(*ahead)
                act.wait_ge(w_ld, 48)
                act.wait_ge(gate_done[b], it + 1)
                act.activation(lg[:, b, bass.ds(it * CH, CH)], ps[0:E, 2 + b, :], ACT.Identity,
                               bias=gbias[:, 0:1]).then_inc(lg_ready[b], 1)
            one_ahead(act, prepare, work)
            for b in range(NB):
                act.wait_ge(nmax_ready, b + 1)
                act.activation(lg[:, b, :], lg[:, b, :], ACT.Exp, bias=nmax[:, b:b + 1],
                               accum_out=gsum[:, b:b + 1]).then_inc(soft_ready, 1)
            for n in range(NB * NCH):
                act.wait_ge(it_done, n + 1)
                act.activation(g.chosen[:, n // NCH, (n % NCH) * CH:(n % NCH + 1) * CH], ps[0:E, 1 + n % 4, :],
                               ACT.Copy).then_inc(it_ready, 1)

        @block.tensor
        def _(pe):
            def transposes(it, b):
                pe.wait_ge(hn_ready[b], it + 1)
                for k in range(KT):
                    pe.wait_ge(ht_ready[1 - b], 2 * it + 2 * b + 1)
                    for t in range(TPC):
                        ins = pe.transpose(ps[:, k, t * P:(t + 1) * P], hn[:, b, t, k * P:(k + 1) * P], g.ident[:, :])
                    ins.then_inc(tr_done[b], 1)

            def work(it, b, ahead):
                if ahead:
                    transposes(*ahead)
                pe.wait_ge(w_ld, 48)
                pe.wait_ge(ht_ready[b], 2 * it + 3)
                pe.wait_ge(lg_ready[b], it + 1)
                for k in range(KT):
                    ins = pe.matmul(ps[0:E, 2 + b, :], gw[:, k, :], hf[:, b, k, :],
                                    start=(k == 0), stop=(k == KT - 1))
                ins.then_inc(gate_done[b], 1)
            one_ahead(pe, transposes, work)
            for b in range(NB):
                pe.wait_ge(pr_ready, b + 1)
                for t in range(NT):
                    o = (b * NT + t) * E
                    ins = pe.transpose(ps[:, 0, o:o + E], lg[:, b, t * P:(t + 1) * P], g.ident[0:E, 0:E])
            ins.then_inc(pt_done, 1)
            pe.wait_ge(ind_ready, 1)
            for n in range(NB * NCH):
                if n >= 4:
                    pe.wait_ge(it_ready, n - 3)
                for t in range(TPC):
                    ins = pe.transpose(ps[0:E, 1 + n % 4, t * P:(t + 1) * P], pn[:, n * TPC + t, :], g.ident[:, :])
                ins.then_inc(it_done, 1)


def phase_experts(nc, g):
    with ExitStack() as c:
        def sb(n, s, d=F32):
            return c.enter_context(nc.sbuf_tensor("ex_" + n, s, d))

        def sem(n):
            return c.enter_context(nc.semaphore("ex_" + n))

        ps = g.ps
        w = sb("w", [P, 2, 3, KT, C])
        bias = sb("bias", [P, 2, 3, KT])
        wb = sb("wb", [P, 2, NB * T])
        one = sb("one", [P, 1, 1])
        one_set = sem("one_set")
        wh = sb("wh", [P, 2, 3, KT, C], F16)
        wl = sb("wl", [P, 2, 3, KT, C], F16)
        hf = [sb(f"hf{l}", [P, KT, CH]) for l in range(2)]
        hh = [sb(f"hh{l}", [P, 2, KT, CH], F16) for l in range(2)]
        hl = [sb(f"hl{l}", [P, 2, KT, CH], F16) for l in range(2)]
        h3 = sb("h3", [P, 2, KT, CH])
        vacc = sb("vacc", [P, 2, KT, NB * NCH])
        vt = sb("vt", [P, E, KT])
        vtk = sb("vtk", [P, KT, E])
        vg = sb("vg", [E, NB, C])
        NC_ = NB * NCH
        NBODY = 2 * NC_
        w_ld = [[sem(f"w_ld{p}{l}") for l in range(3)] for p in range(2)]
        ld = [sem(f"ld{p}") for p in range(2)]
        ready = [sem(f"ready{l}") for l in range(3)]
        w_high = [sem(f"w_high{p}") for p in range(2)]
        w_split = [sem(f"w_split{p}") for p in range(2)]
        high = [sem(f"high{l}") for l in range(2)]
        act_h = [sem(f"act_h{l}") for l in range(2)]
        dve_h = [sem(f"dve_h{l}") for l in range(2)]
        dve_y, act_v = sem("dve_y"), sem("act_v")
        vt_done = [sem(f"vt_done{p}") for p in range(2)]
        chain_s, v_tr, v_ready, o_ready, x_done = (sem("chain"), sem("v_tr"), sem("v_ready"), sem("o_ready"),
                                                   sem("x_done"))
        SEQ = [(l, s - l) for s in range(NBODY + 2) for l in range(3) if 0 <= s - l < NBODY]
        PAIR = {key: n % 4 for n, key in enumerate(SEQ)}
        NLD = 2
        block = c.enter_context(nc.Block())

        @block.sync
        def _(sp):
            for s in (*vt_done, *act_h, *dve_h, dve_y, act_v):
                sp.sem_inc(s, 1)
            with sp.Fori(0, E // 2) as it:
                for p in range(2):
                    e = it * 2 + p
                    sp.wait_ge(vt_done[p], it + 1)
                    for l, src in enumerate((g.i["w1"], g.i["w2"], g.i["w3"])):
                        sp.dma_start(w[:, p, l], src[bass.ds(e, 1)].rearrange("e (k p) o -> p (e k) o", p=P))\
                          .then_inc(w_ld[p][l], 16)
                    sp.dma_start(bias[:, p], g.i["b"][bass.ds(e, 1)].rearrange("e p l k -> p (e l) k"))\
                      .then_inc(ld[p], 16)
                    sp.dma_start(wb[:, p, :], g.d_wt[bass.ds(e, 1), :].to_broadcast([P, NB * T])).then_inc(ld[p], 16)

        @block.gpsimd
        def _(pool):
            pool.memset(one[:, :, :], 1.0).then_inc(one_set, 1)
            pool.wait_ge(one_set, 1)
            with pool.Fori(0, E // 2) as it:
                for p in range(2):
                    for l in range(3):
                        pool.wait_ge(w_ld[p][l], (it + 1) * 16)
                        pool.tensor_tensor(wh[:, p, l], w[:, p, l], one[:, :, :].to_broadcast([P, KT, C]), ALU.mult)\
                            .then_inc(w_high[p], 1)
                        pool.wait_ge(w_high[p], it * 3 + l + 1)
                        pool.tensor_tensor(wl[:, p, l], w[:, p, l], wh[:, p, l], ALU.subtract).then_inc(w_split[p], 1)

        @block.tensor
        def _(pe):
            with pe.Fori(0, E // 2) as it:
                for n, (l, cc) in enumerate(SEQ):
                    p, chunk = cc // NC_, cc % NC_
                    if chunk == 0:
                        pe.wait_ge(w_split[p], it * 3 + l + 1)
                    left = [0 if n == 0 else None] * 3
                    if n >= 4:
                        left[SEQ[n - 4][0]] = SEQ[n - 4][1] + 1
                    if l:
                        pe.wait_ge(dve_h[l - 1], it * NBODY + cc + 2)
                    for m in range(3):
                        if left[m] is None:
                            continue
                        if m < 2:
                            pe.wait_ge(act_h[m], it * NBODY + left[m] + 1)
                        else:
                            pe.wait_ge(dve_y, it * NBODY + left[m] + 1)
                    if l == 0:
                        xh, xl = (t[:, :, chunk * CH:(chunk + 1) * CH] for t in (g.hh, g.hl))
                    else:
                        xh, xl = hh[l - 1][:, cc % 2], hl[l - 1][:, cc % 2]
                    for o in range(KT):
                        parts = [(a[:, p, l, k, o * P:(o + 1) * P], x[:, k, :]) for k in range(KT)
                                 for a, x in ((wh, xh), (wl, xh), (wh, xl))]
                        for i, (lhs, rhs) in enumerate(parts):
                            ins = pe.matmul(ps[:, 2 * PAIR[l, cc] + o, :], lhs, rhs, start=(i == 0),
                                            stop=(i == len(parts) - 1))
                    ins.then_inc(ready[l], 1)
            pe.wait_ge(v_ready, 1)
            for k in range(KT):
                ins = pe.transpose(ps[0:E, 0, k * P:(k + 1) * P], vtk[:, k, :], g.ident[:, :])
            ins.then_inc(v_tr, 1)
            for n in range(NB * NT // 2):
                b = n // (NT // 2)
                pe.wait_ge(v_ready, 2 + b)
                if n >= 4:
                    pe.wait_ge(x_done, n - 3)
                for t in range(2):
                    tt = 2 * n + t - b * NT
                    ins = pe.matmul(ps[:, 1 + n % 4, t * C:(t + 1) * C], g.chosen[:, b, tt * P:(tt + 1) * P], vg[:, b, :],
                                    start=True, stop=True)
                ins.then_inc(o_ready, 1)

        @block.scalar
        def _(act):
            with act.Fori(0, E // 2) as it:
                for s in range(NBODY + 3):
                    if s % NC_ == 0 and s < NBODY:
                        act.wait_ge(ld[s // NC_], (it + 1) * (16 * NLD))
                    for l in range(2):
                        cc = s - l
                        if 0 <= cc < NBODY:
                            act.wait_ge(ready[l], it * NBODY + cc + 1)
                            act.wait_ge(dve_h[l], it * NBODY + cc + 1)
                            for o in range(KT):
                                ins = act.activation(hf[l][:, o, :], ps[:, 2 * PAIR[l, cc] + o, :], ACT.Relu,
                                                     bias=bias[:, cc // NC_, l, o:o + 1])
                            ins.then_inc(act_h[l], 1)
                    cc = s - 3
                    if 0 <= cc < NBODY:
                        p = cc // NC_
                        if cc % NC_ == 0:
                            act.wait_ge(vt_done[p], it + 1)
                        act.wait_ge(dve_y, it * NBODY + cc + 2)
                        for o in range(KT):
                            ins = act.activation(h3[:, cc % 2, o, :], h3[:, cc % 2, o, :], ACT.Relu,
                                                 accum_out=vacc[:, p, o, cc % NC_:cc % NC_ + 1])
                        ins.then_inc(act_v, 1)

        @block.vector
        def _(dve):
            ch = Chain(dve, chain_s)
            with dve.Fori(0, E // 2) as it:
                for s in range(NBODY + 4):
                    for l in range(2):
                        cc = s - l
                        if 0 <= cc < NBODY:
                            dve.wait_ge(act_h[l], it * NBODY + cc + 2)
                            dve.tensor_copy(hh[l][:, cc % 2], hf[l][:, :, :]).then_inc(high[l], 1)
                            dve.wait_ge(high[l], it * NBODY + cc + 1)
                            dve.tensor_tensor(hl[l][:, cc % 2], hf[l][:, :, :], hh[l][:, cc % 2], ALU.subtract)\
                               .then_inc(dve_h[l], 1)
                    cc = s - 2
                    if 0 <= cc < NBODY:
                        p, chunk = cc // NC_, cc % NC_
                        dve.wait_ge(ready[2], it * NBODY + cc + 1)
                        dve.wait_ge(act_v, it * NBODY + max(cc - 1, 0) + 1)
                        for o in range(KT):
                            ins = dve.scalar_tensor_tensor(h3[:, cc % 2, o, :], ps[:, 2 * PAIR[2, cc] + o, :],
                                                           bias[:, p, 2, o:o + 1], wb[:, p, chunk * CH:(chunk + 1) * CH],
                                                           ALU.add, ALU.mult)
                        ins.then_inc(dve_y, 1)
                    cc = s - 4
                    if 0 <= cc < NBODY and cc % NC_ == NC_ - 1:
                        p = cc // NC_
                        dve.wait_ge(act_v, it * NBODY + cc + 2)
                        dve.tensor_reduce(vt[:, bass.ds(it * 2 + p, 1), :].rearrange("p e k -> p (e k)"),
                                          vacc[:, p], AX.X, ALU.add).then_inc(vt_done[p], 1)
            dve.wait_ge(vt_done[1], E // 2 + 1)
            dve.tensor_copy(vtk[:, :, :], vt[:, :, :].rearrange("p e k -> p k e")).then_inc(v_ready, 1)
            dve.wait_ge(v_tr, 1)
            for b in range(NB):
                dve.tensor_tensor(vg[:, b, :], ps[0:E, 0, 0:C], g.gb0[:, b, :], ALU.mult).then_inc(v_ready, 1)
            for n in range(NB * NT // 2):
                dve.wait_ge(o_ready, n + 1)
                xs = g.x[:, 2 * n:2 * n + 2, :]
                dve.tensor_tensor(xs, xs, ps[:, 1 + n % 4, :].rearrange("p (t c) -> p t c", t=2), ALU.add)\
                   .then_inc(x_done, 1)


def phase_mix(nc, g):
    with ExitStack() as c:
        def sb(n, s, d=F32):
            return c.enter_context(nc.sbuf_tensor("mi_" + n, s, d))

        def sem(n):
            return c.enter_context(nc.semaphore("mi_" + n))

        ps = g.ps
        hn = sb("hn", [P, NB, TPC, C])
        ht = sb("ht", [P, NB, KT, CH])
        wa = sb("wa", [P, KT, NH])
        wv = sb("wv", [P, KT, C])
        vn = sb("vn", [P, NB * NT, C])
        z = sb("z", [NH, NB, T])
        zero = sb("zero", [NH, NB, P])
        nmax = sb("nmax", [NH, NB])
        zsum = sb("zsum", [NH, NB])
        zrec = sb("zrec", [NH, NB])
        w_ld, chain_s = sem("w_ld"), sem("chain")
        ln = LayerNorm(sb, sem)
        hn_ready = [sem(f"hn_ready{b}") for b in range(NB)]
        tr_done = [sem(f"tr_done{b}") for b in range(NB)]
        ht_ready = [sem(f"ht_ready{b}") for b in range(NB)]
        z_done = [sem(f"z_done{b}") for b in range(NB)]
        z_ready = [sem(f"z_ready{b}") for b in range(NB)]
        v_done = [sem(f"v_done{b}") for b in range(NB)]
        v_ready = [sem(f"v_ready{b}") for b in range(NB)]
        nmax_ready, exp_ready, zn_ready, zstored = sem("nmax_ready"), sem("exp_ready"), sem("zn_ready"), sem("zstored")
        tz = sb("tz", [P, 2, NB, T])
        toep_ld = [[sem(f"toep_ld{p}{b}") for b in range(NB)] for p in range(2)]
        mix_done = [[sem(f"mix_done{p}{b}") for b in range(NB)] for p in range(2)]
        mix_read = [[sem(f"mix_read{p}{b}") for b in range(NB)] for p in range(2)]
        block = c.enter_context(nc.Block())

        @block.gpsimd
        def _(pool):
            pool.memset(zero[:, :, :], 0.0).then_inc(zn_ready, 1)

        @block.sync
        def _(sp):
            for s in (*mix_done[0], *mix_done[1], *tr_done, *ht_ready, *z_ready, *v_ready, *mix_read[0], *mix_read[1]):
                sp.sem_inc(s, 1)
            sp.dma_start(wa[:, :, :], g.i["wa"].rearrange("(k p) h -> p k h", p=P)).then_inc(w_ld, 16)
            sp.dma_start(wv[:, :, :], g.i["wv"].rearrange("(k p) n -> p k n", p=P)).then_inc(w_ld, 16)
            sp.wait_ge(zn_ready, 1 + NB)
            sp.dma_start(g.d_z[:, :, 0:P], zero[:, :, :]).then_inc(zstored, 16)
            sp.dma_start(g.d_z[:, :, P:], z[:, :, :]).then_inc(zstored, 16)
            sp.wait_ge(zstored, 32)
            with sp.Fori(0, NH // 2) as it:
                for p in range(2):
                    for b in range(NB):
                        sp.wait_ge(mix_done[p][b], it + 1)
                        row = g.d_z[bass.ds(it * 2 + p, 1), b, 1:1 + T]
                        src = bass.AP(row.tensor, row.offset, [[1, P], [1, T]])
                        sp.dma_start(tz[:, p, b, :], src).then_inc(toep_ld[p][b], 16)

        @block.vector
        def _(dve):
            ch = Chain(dve, chain_s)

            def normalise(it, b):
                ch.at((it * NB + b) * LN_LINKS)
                dve.wait_ge(tr_done[b], 2 * it + 1)
                ln_rows(dve, ch, g.x, b * NT + it * TPC, hn[:, b], ln, b, it).then_inc(hn_ready[b], 1)

            def work(it, b, ahead):
                if ahead:
                    normalise(*ahead)
                if not isinstance(it, int):
                    values(it, b)

            def values(it, b):
                for j in range(2):
                    dve.wait_ge(v_done[b], 2 * it + j + 1)
                    dve.tensor_copy(vn[:, bass.ds(b * NT + it * TPC + 2 * j, 2), :],
                                    ps[:, 4 + 2 * b + j, :].rearrange("p (t c) -> p t c", t=2)).then_inc(v_ready[b], 1)
            one_ahead(dve, normalise, work)
            ch.at(NCH * NB * LN_LINKS)
            for b in range(NB):
                dve.wait_ge(z_ready[b], NCH + 1)
                ins = dve.tensor_reduce(nmax[:, b:b + 1], z[:, b, :], AX.X, ALU.max, negate=True)
                ins.then_inc(nmax_ready, 1)
            dve.wait_ge(exp_ready, NB)
            ch.link(dve.reciprocal(zrec[:, :], zsum[:, :]))
            for b in range(NB):
                dve.tensor_scalar(z[:, b, :], z[:, b, :], zrec[:, b:b + 1], None, ALU.mult).then_inc(zn_ready, 1)
            for b in range(NB):
                values(NCH - 1, b)
            with dve.Fori(0, NH // 2) as it:
                for p in range(2):
                    for b in range(NB):
                        dve.wait_ge(mix_done[p][b], it + 2)
                        dve.tensor_copy(g.mixed[:, b * NT:(b + 1) * NT, bass.ds((it * 2 + p) * HD, HD)],
                                        ps[:, 2 * p + b, 0:C].rearrange("p (t d) -> p t d", d=HD))\
                           .then_inc(mix_read[p][b], 1)

        @block.scalar
        def _(act):
            def prepare(it, b):
                ln_root(act, ln, g.eps, b, it)
                for k in range(KT):
                    act.wait_ge(tr_done[b], 2 * it + k + 2)
                    act.activation(backwards(ht[:, b, k, :]), ps[:, k, :].rearrange("p (t n) -> p t n", n=P),
                                   ACT.Identity, scale=g.mod[:, 1, 1, k, b:b + 1],
                                   bias=g.mod[:, 1, 0, k, b:b + 1]).then_inc(ht_ready[b], 1)

            def work(it, b, ahead):
                if ahead:
                    prepare(*ahead)
                act.wait_ge(z_done[b], it + 1)
                act.activation(z[:, b, bass.ds(it * CH, CH)].rearrange("h (t n) -> h t n", n=P),
                               backwards(ps[0:NH, 2 + b, :]), ACT.Copy,
                               scale=float(HD) ** -0.5).then_inc(z_ready[b], 1)
            one_ahead(act, prepare, work)
            for b in range(NB):
                act.wait_ge(nmax_ready, b + 1)
                act.activation(z[:, b, :], z[:, b, :], ACT.Exp, bias=nmax[:, b:b + 1],
                               accum_out=zsum[:, b:b + 1]).then_inc(exp_ready, 1)

        @block.tensor
        def _(pe):
            def transposes(it, b):
                pe.wait_ge(hn_ready[b], it + 1)
                for k in range(KT):
                    pe.wait_ge(ht_ready[1 - b], 2 * it + 2 * b + 1)
                    for t in range(TPC):
                        ins = pe.transpose(ps[:, k, t * P:(t + 1) * P], hn[:, b, t, k * P:(k + 1) * P], g.ident[:, :])
                    ins.then_inc(tr_done[b], 1)

            def work(it, b, ahead):
                pe.wait_ge(w_ld, 32)
                pe.wait_ge(ht_ready[b], 2 * it + 3)
                pe.wait_ge(z_ready[b], it + 1)
                for k in range(KT):
                    ins = pe.matmul(ps[0:NH, 2 + b, :], wa[:, k, :], ht[:, b, k, :], start=(k == 0), stop=(k == KT - 1))
                ins.then_inc(z_done[b], 1)
                if isinstance(it, int):
                    if ahead:
                        transposes(*ahead)
                else:
                    values(it, b, ahead)

            def values(it, b, ahead):
                for j in range(2):
                    if j == 1 and ahead:
                        transposes(*ahead)
                    pe.wait_ge(v_ready[b], 2 * it + j + 1)
                    for t in range(2):
                        tok = (2 * j + t) * P
                        for k in range(KT):
                            ins = pe.matmul(ps[:, 4 + 2 * b + j, t * C:(t + 1) * C], ht[:, b, k, tok:tok + P],
                                            wv[:, k, :], start=(k == 0), stop=(k == KT - 1))
                    ins.then_inc(v_done[b], 1)
            one_ahead(pe, transposes, work)
            for b in range(NB):
                values(NCH - 1, b, None)
            for b in range(NB):
                pe.wait_ge(v_ready[b], 2 * NCH + 1)
            with pe.Fori(0, NH // 2) as it:
                for p in range(2):
                    for b in range(NB):
                        pe.wait_ge(toep_ld[p][b], (it + 1) * 16)
                        pe.wait_ge(mix_read[p][b], it + 1)
                        for d in range(NT):
                            ins = pe.matmul(ps[:, 2 * p + b, d * HD:C], tz[:, p, b, d * P:(d + 1) * P],
                                            vn[:, b * NT:(b + 1) * NT - d, bass.ds((it * 2 + p) * HD, HD)],
                                            start=(d == 0), stop=(d == NT - 1))
                        ins.then_inc(mix_done[p][b], 1)


def phase_mix_out(nc, g):
    with ExitStack() as c:
        def sem(n):
            return c.enter_context(nc.semaphore("mo_" + n))

        ps = g.ps
        at = c.enter_context(nc.sbuf_tensor("mo_at", [P, 2, KT, CH], F32))
        st = c.enter_context(nc.sbuf_tensor("mo_st", [P, NB * NT, 6], F32))
        sd = c.enter_context(nc.sbuf_tensor("mo_sd", [P, NB * NT], F32))
        tr_done, at_ready, o_ready, x_done = sem("tr_done"), sem("at_ready"), sem("o_ready"), sem("x_done")
        st_done, var_ready, root_ready = sem("st_done"), sem("var_ready"), sem("root_ready")
        N = NB * NCH
        block = c.enter_context(nc.Block())

        @block.tensor
        def _(pe):
            def turn(n):
                for k in range(KT):
                    if n:
                        pe.wait_ge(at_ready, KT * (n - 1) + k + 1)
                    for t in range(TPC):
                        ins = pe.transpose(ps[:, k, t * P:(t + 1) * P], g.mixed[:, n * TPC + t, k * P:(k + 1) * P],
                                           g.ident[:, :])
                    ins.then_inc(tr_done, 1)

            turn(0)
            for n in range(N):
                b = n // NCH
                if n + 1 < N:
                    turn(n + 1)
                pe.wait_ge(at_ready, KT * (n + 1))
                for j in range(2):
                    m = 2 * n + j
                    if m >= 4:
                        pe.wait_ge(x_done, m - 3)
                    for t in range(2):
                        tok = (2 * j + t) * P
                        out = ps[:, 2 + m % 4, t * C:(t + 1) * C]
                        for k in range(KT):
                            pe.matmul(out, at[:, n % 2, k, tok:tok + P], g.wo1g[:, b, k, :], start=(k == 0), stop=False)
                        ins = pe.matmul(out, g.ones1[:, :], g.bo1g[:, b, :], start=False, stop=True)
                    ins.then_inc(o_ready, 1)

        @block.scalar
        def _(act):
            for n in range(N):
                if n >= 2:
                    act.wait_ge(o_ready, 2 * (n - 1))
                for k in range(KT):
                    act.wait_ge(tr_done, KT * n + k + 1)
                    act.activation(at[:, n % 2, k, :], ps[:, k, :], ACT.Copy).then_inc(at_ready, 1)
            act.wait_ge(var_ready, 1)
            act.activation(sd[:, :], g.mv[:, :, 1], ACT.Sqrt, bias=g.eps[:, 0:1]).then_inc(root_ready, 1)

        @block.vector
        def _(dve):
            for m in range(2 * N):
                dve.wait_ge(o_ready, m + 1)
                xs = g.x[:, 2 * m:2 * m + 2, :]
                dve.tensor_tensor(xs, xs, ps[:, 2 + m % 4, :].rearrange("p (t c) -> p t c", t=2), ALU.add)\
                   .then_inc(x_done, 1)
                dve.wait_ge(x_done, m + 1)
                for t in range(2 * m, 2 * m + 2):
                    ins = dve.bn_stats(st[:, t, :], g.x[:, t, :])
            ins.then_inc(st_done, 1)
            dve.wait_ge(st_done, 1)
            for t in range(NB * NT):
                ins = dve.bn_aggr(g.mv[:, t, :], st[:, t, :])
            ins.then_inc(var_ready, 1)
            dve.wait_ge(root_ready, 1)
            dve.reciprocal(g.rs[:, :], sd[:, :])


def phase_ffn(nc, g):
    with ExitStack() as c:
        def sb(n, s, d=F32):
            return c.enter_context(nc.sbuf_tensor("ff_" + n, s, d))

        def sem(n):
            return c.enter_context(nc.semaphore("ff_" + n))

        ps = g.ps
        hn = sb("hn", [P, NB, TPC, C])
        ht = sb("ht", [P, NB, KT, CH + 1])
        wr = sb("wr", [P, KT, C])
        wk = sb("wk", [P, KT, C])
        mu = sb("mu", [P, 2, KT])
        omu = sb("omu", [P, 2, KT])
        xp = sb("xp", [P, 2, KT, CH])
        xm = sb("xm", [P, NB, 2, KT, CH])
        r = sb("r", [P, NB, TPC, C])
        kr = sb("kr", [P, NB, KT, CH])
        ka = sb("ka", [P, NB, KT, CH])
        y = sb("y", [P, NB, TPC, C])
        w_ld, chain_m, chain_y, zero_done = sem("w_ld"), sem("chain_m"), sem("chain_y"), sem("zero_done")
        hn_ready = [sem(f"hn_ready{b}") for b in range(NB)]
        tr_done = [sem(f"tr_done{b}") for b in range(NB)]
        ht_ready = [sem(f"ht_ready{b}") for b in range(NB)]
        xm_ready = [sem(f"xm_ready{b}") for b in range(NB)]
        r_done = [sem(f"r_done{b}") for b in range(NB)]
        r_ready = [sem(f"r_ready{b}") for b in range(NB)]
        k_done = [sem(f"k_done{b}") for b in range(NB)]
        kr_ready = [sem(f"kr_ready{b}") for b in range(NB)]
        ka_ready = [sem(f"ka_ready{b}") for b in range(NB)]
        v_done = [sem(f"v_done{b}") for b in range(NB)]
        y_ready = [sem(f"y_ready{b}") for b in range(NB)]
        stored = [sem(f"stored{b}") for b in range(NB)]
        block = c.enter_context(nc.Block())

        @block.gpsimd
        def _(pool):
            pool.memset(ht[:, :, :, CH:CH + 1], 0.0).then_inc(zero_done, 1)
            with pool.Fori(0, NCH) as it:
                for b in range(NB):
                    pool.wait_ge(v_done[b], 2 * it + 1)
                    for k in range(KT):
                        pool.wait_ge(kr_ready[b], 2 * it + k + 2)
                        pool.tensor_tensor(ka[:, b, k, :], kr[:, b, k, :], kr[:, b, k, :], ALU.mult)\
                            .then_inc(ka_ready[b], 1)

        @block.sync
        def _(sp):
            for s in (*tr_done, *v_done, *stored, *xm_ready, *kr_ready, *r_ready, *y_ready, *ht_ready):
                sp.sem_inc(s, 1)
            sp.dma_start(wr[:, :, :], g.i["wr"].rearrange("(k p) n -> p k n", p=P)).then_inc(w_ld, 16)
            sp.dma_start(wk[:, :, :], g.i["wk"].rearrange("(k p) n -> p k n", p=P)).then_inc(w_ld, 16)
            sp.dma_start(mu[:, :, :], g.i["mu"]).then_inc(w_ld, 16)
            with sp.Fori(0, NCH) as it:
                for b in range(NB):
                    sp.wait_ge(y_ready[b], 2 * it + 3)
                    sp.dma_start(g.out[bass.ds(b * T + it * CH, CH), :].rearrange("(t p) c -> p t c", p=P), y[:, b])\
                      .then_inc(stored[b], 16)
            for b in range(NB):
                sp.wait_ge(stored[b], 16 * NCH + 1)

        @block.vector
        def _(dve):
            ch, chm = Chain(dve, chain_y), Chain(dve, chain_m)
            def normalise(it, b):
                dve.wait_ge(tr_done[b], 2 * it + 1)
                for t in range(TPC):
                    tile = b * NT + it * TPC + t
                    ins = dve.tensor_scalar(hn[:, b, t, :], g.x[:, tile, :], g.mv[:, tile, 0:1], g.rs[:, bass.ds(tile, 1)],
                                            ALU.subtract, ALU.mult)
                ins.then_inc(hn_ready[b], 1)

            def mix(it, b):
                chm.at(it * NB + b + 1)
                dve.wait_ge(ht_ready[b], 3 * it + 4)
                for q in range(2):
                    for k in range(KT):
                        ins = dve.tensor_scalar(xp[:, q, k, :], ht[:, b, k, 0:CH], omu[:, q, k:k + 1], None, ALU.mult)
                chm.link(ins)
                for q in range(2):
                    for k in range(KT):
                        ins = dve.scalar_tensor_tensor(xm[:, b, q, k, :], ht[:, b, k, 1:CH + 1], mu[:, q, k:k + 1],
                                                       xp[:, q, k, :], ALU.mult, ALU.add)
                ins.then_inc(xm_ready[b], 1)

            def start(it, b):
                normalise(it, b)
                dve.wait_ge(w_ld, 48)
                chm.link(dve.tensor_scalar(omu[:, :, :], mu[:, :, :], -1.0, 1.0, ALU.mult, ALU.add))
                mix(it, b)

            def work(it, b, ahead):
                if ahead:
                    normalise(*ahead)
                    mix(*ahead)
                ch.at((it * NB + b) * 2)
                dve.wait_ge(stored[b], 16 * it + 1)
                for j in range(2):
                    dve.wait_ge(r_ready[b], 2 * it + j + 2)
                    dve.wait_ge(v_done[b], 2 * it + j + 2)
                    ys = y[:, b, 2 * j:2 * j + 2, :]
                    ch.link(dve.tensor_tensor(ys, r[:, b, 2 * j:2 * j + 2, :],
                                              ps[:, 4 + j, :].rearrange("p (t c) -> p t c", t=2), ALU.mult))
                    dve.tensor_tensor(ys, ys, g.x[:, bass.ds(b * NT + it * TPC + 2 * j, 2), :], ALU.add)\
                       .then_inc(y_ready[b], 1)
            one_ahead(dve, start, work)

        @block.scalar
        def _(act):
            act.wait_ge(zero_done, 1)

            def modulated(it, b):
                act.wait_ge(xm_ready[b], it + 1)
                act.activation(ht[:, b, :, 0:1], ht[:, b, :, CH:CH + 1], ACT.Copy).then_inc(ht_ready[b], 1)
                act.wait_ge(ht_ready[b], 3 * it + 2)
                for k in range(KT):
                    act.wait_ge(tr_done[b], 2 * it + k + 2)
                    act.activation(ht[:, b, k, 1:CH + 1], ps[:, k, :], ACT.Identity, scale=g.mod[:, 1, 3, k, b:b + 1],
                                   bias=g.mod[:, 1, 2, k, b:b + 1]).then_inc(ht_ready[b], 1)

            def work(it, b, ahead):
                for k in range(KT):
                    act.wait_ge(k_done[b], 2 * it + k + 1)
                    act.activation(kr[:, b, k, :], ps[:, 2 + k, :], ACT.Relu).then_inc(kr_ready[b], 1)
                if ahead:
                    modulated(*ahead)
                for j in range(2):
                    act.wait_ge(r_done[b], 2 * it + j + 1)
                    act.activation(r[:, b, 2 * j:2 * j + 2, :], ps[:, 6 + j, :].rearrange("p (t c) -> p t c", t=2),
                                   ACT.Sigmoid).then_inc(r_ready[b], 1)
            one_ahead(act, modulated, work)

        @block.tensor
        def _(pe):
            def transposes(it, b):
                pe.wait_ge(hn_ready[b], it + 1)
                for k in range(KT):
                    pe.wait_ge(ht_ready[1 - b], 3 * it + 3 * b + 1)
                    for t in range(TPC):
                        ins = pe.transpose(ps[:, k, t * P:(t + 1) * P], hn[:, b, t, k * P:(k + 1) * P], g.ident[:, :])
                    ins.then_inc(tr_done[b], 1)

            def work(it, b, ahead):
                o = 1 - b
                pe.wait_ge(w_ld, 48)
                pe.wait_ge(xm_ready[b], it + 2)
                pe.wait_ge(kr_ready[o], 2 * it + 2 * b + 1)
                for q in range(KT):
                    for k in range(KT):
                        ins = pe.matmul(ps[:, 2 + q, :], wk[:, k, q * P:(q + 1) * P], xm[:, b, 1, k, :],
                                        start=(k == 0), stop=(k == KT - 1))
                    ins.then_inc(k_done[b], 1)
                if ahead:
                    transposes(*ahead)
                pe.wait_ge(r_ready[o], 2 * it + 2 * b + 1)
                for j in range(2):
                    for t in range(2):
                        tok = (2 * j + t) * P
                        for k in range(KT):
                            ins = pe.matmul(ps[:, 6 + j, t * C:(t + 1) * C], xm[:, b, 0, k, tok:tok + P],
                                            wr[:, k, :], start=(k == 0), stop=(k == KT - 1))
                    ins.then_inc(r_done[b], 1)
                pe.wait_ge(ka_ready[b], 2 * it + 2)
                pe.wait_ge(y_ready[o], 2 * it + 2 * b + 1)
                for j in range(2):
                    for t in range(2):
                        tok = (2 * j + t) * P
                        for k in range(KT):
                            ins = pe.matmul(ps[:, 4 + j, t * C:(t + 1) * C], ka[:, b, k, tok:tok + P],
                                            g.wv1g[:, b, k, :], start=(k == 0), stop=(k == KT - 1))
                    ins.then_inc(v_done[b], 1)
            one_ahead(pe, transposes, work)


PHASES = (phase_setup, phase_project, phase_attention, phase_route, phase_experts, phase_mix, phase_mix_out, phase_ffn)


def adaln_two_layers(nc, args, out):
    g = Shared(args, out)
    with ExitStack() as c:
        def sb(n, s, d=F32):
            return c.enter_context(nc.sbuf_tensor(n, s, d))

        def dram(n, s, d):
            return nc.dram_tensor(n, s, d).ap()

        g.ps = c.enter_context(nc.psum_tensor("ps", [P, 8, 512], F32))
        g.x = sb("x", [P, NB * NT, C])
        g.ident = sb("ident", [P, P])
        g.identb = sb("identb", [P, P], BF16)
        g.maskb = sb("maskb", [P, 2, P], BF16)
        g.ones1 = sb("ones1", [1, P])
        g.eps = sb("eps", [P, 1])
        g.mv = sb("mv_all", [P, NB * NT, 2])
        g.rs = sb("rs_all", [P, NB * NT])
        g.mod = sb("mod", [P, 2, 4, KT, NB])
        g.wog = sb("wog", [P, NB, NG, C])
        g.wo1g = sb("wo1g", [P, NB, KT, C])
        g.wv1g = sb("wv1g", [P, NB, KT, C])
        g.bo1g = sb("bo1g", [1, NB, C])
        g.gb0 = sb("gb0", [E, NB, C])
        g.d_qh, g.d_ql = dram("d_qh", [C, NB * T], F16), dram("d_ql", [C, NB * T], F16)
        g.d_kh, g.d_kl = dram("d_kh", [C, NB * T], F16), dram("d_kl", [C, NB * T], F16)
        g.d_qrh = dram("d_qrh", [DR, NB * T], F16)
        g.d_krh = dram("d_krh", [DR, NB * T], F16)
        g.d_va = dram("d_va", [P, NB * NT, NH * 32], F32)
        g.d_wt = dram("d_wt", [E, NB * T], F32)
        g.d_z = dram("d_z", [NH, NB, P + T], F32)
        phase_setup(nc, g)
        with ExitStack() as a:
            g.bq = a.enter_context(nc.sbuf_tensor("bq", [P, NB, T], F16))
            g.bk = a.enter_context(nc.sbuf_tensor("bk", [P, NB, T], F16))
            phase_project(nc, g)
            phase_attention(nc, g)
        with ExitStack() as a:
            g.hh = a.enter_context(nc.sbuf_tensor("hh_all", [P, KT, NB * T], F16))
            g.hl = a.enter_context(nc.sbuf_tensor("hl_all", [P, KT, NB * T], F16))
            g.chosen = a.enter_context(nc.sbuf_tensor("chosen", [E, NB, T], F32))
            phase_route(nc, g)
            phase_experts(nc, g)
        with ExitStack() as a:
            g.mixed = a.enter_context(nc.sbuf_tensor("mixed", [P, NB * NT, C], F32))
            phase_mix(nc, g)
            phase_mix_out(nc, g)
        phase_ffn(nc, g)


def constants():
    i = np.arange(P)
    mask = np.stack([np.where(i[:, None] > i[None, :], NEG, 0.0), np.where(i[None, :] > i[:, None], NEG, 0.0)], 1)
    inv = (1.0 / 10000.0 ** (np.arange(0, DR, 2, dtype=np.float32) / np.float32(DR))).astype(np.float32)
    ang = np.outer(np.arange(T, dtype=np.float32), inv).astype(np.float32)
    cos, sin = np.cos(ang).T, np.sin(ang).T
    cs = np.concatenate([cos, cos, cos, cos, -sin, sin, -sin, sin], 0)
    before = np.broadcast_to(np.arange(E)[None, :] < np.arange(E)[:, None], (P, E, E))
    return {"ident": np.eye(P), "mask": mask, "cs": cs, "before": before}


def layout(w):
    half = DR // 2

    def rope_cols(a):
        s = np.concatenate([a[:, half:], a[:, :half]], 1)
        return np.concatenate([a, a, s, s], 1)

    wo = np.zeros((NG, HG, 32, C), np.float32)
    wo[:, :, :HD] = w["L0_attn_W_o"].reshape(NG, HG, HD, C)
    cT = np.stack([w["L0_c"].T.reshape(KT, P, NB), w["L1_c"].T.reshape(KT, P, NB)]).transpose(2, 0, 1, 3)
    b = np.stack([w["L0_ffn_b1"], w["L0_ffn_b2"], w["L0_ffn_b3"]], 1).reshape(E, 3, KT, P).transpose(0, 3, 1, 2)
    mu = np.stack([w["L1_ffn_mu_r"], w["L1_ffn_mu_k"]]).reshape(2, KT, P).transpose(2, 0, 1)
    return {
        "x": w["L0_attn_x"].reshape(NB * T, C), "cT": cT, "wmod0": w["L0_wmod"], "wmod1": w["L1_wmod"],
        "wkv": w["L0_attn_W_kv_down"], "wq": w["L0_attn_W_q"], "wqr": rope_cols(w["L0_attn_W_q_rope"]),
        "wkr": rope_cols(w["L0_attn_W_k_rope"]), "wku": w["L0_attn_W_k_up"], "wvu": w["L0_attn_W_v_up"],
        "wo0": wo.reshape(NG, P, C), "gw": w["L0_ffn_gate_w"], "gb": w["L0_ffn_gate_b"].reshape(E, 1),
        "w1": w["L0_ffn_w1"], "w2": w["L0_ffn_w2"], "w3": w["L0_ffn_w3"], "b": b,
        "wa": w["L1_attn_W_A"].T, "wv": w["L1_attn_W_V"].T, "wo1": w["L1_attn_W_O"].T,
        "bo1": w["L1_attn_b_O"].reshape(1, C), "wr": w["L1_ffn_W_r"].T, "wk": w["L1_ffn_W_k"].T,
        "wv1": w["L1_ffn_W_v"].T, "mu": mu,
    }


def kernel(**inputs):
    import concourse.bacc as bacc
    from concourse.bass_utils import run_bass_kernel_spmd

    nc = bacc.Bacc("TRN2", target_bir_lowering=False, num_devices=1)
    host = layout({k: np.asarray(v) for k, v in inputs.items()})
    host.update({k: v.astype(np.float32) for k, v in constants().items()})
    arrays, args = {}, {}
    for name, a in host.items():
        arrays["in_" + name] = np.ascontiguousarray(a)
        args[name] = nc.dram_tensor("in_" + name, a.shape, F32, kind="ExternalInput").ap()
    out = nc.dram_tensor("out", (NB * T, C), F32, kind="ExternalOutput").ap()
    adaln_two_layers(nc, args, out)
    r = run_bass_kernel_spmd(nc, [arrays], core_ids=[0])
    return r.results[0]["out"].reshape(NB, T, C)
```
